# Optimizing a Trainium2 kernel written in Bass

```python
import numpy as np
import jax
import jax.numpy as jnp

def _softmax(x, axis=-1):
    return jax.nn.softmax(x, axis=axis)

def _gelu(x):
    return jax.nn.gelu(x, approximate=True)

def _silu(x):
    return jax.nn.silu(x)

def _sigmoid(x):
    return jax.nn.sigmoid(x)

def _layernorm(x, axis=-1, eps=1e-05):
    m = jnp.mean(x, axis=axis, keepdims=True)
    v = jnp.var(x, axis=axis, keepdims=True)
    return (x - m) / jnp.sqrt(v + eps)

def _scatter_add(tgt, idx, src, axis=0):
    return tgt.at[idx].add(src)

def _segment_sum(src, seg, n):
    return jax.ops.segment_sum(src, seg, n)
kernel_name = 'mk_gnn_preln_d4_gnn_r8_bb3ce4'

def setup_inputs(seed: int=0):
    np.random.seed(seed)
    _w = jnp.asarray

    def _rec_inputs():
        import jax
        import jax.numpy as jnp
        _gk = jax.random.key(seed)
        x = -0.000202 + 1 * jax.random.normal(jax.random.fold_in(_gk, 1), (6250, 64), jnp.float32)
        _s = jax.random.randint(jax.random.fold_in(_gk, 2), (100000,), 0, 6250, jnp.int32)
        _d = jax.random.randint(jax.random.fold_in(_gk, 3), (100000,), 0, 6250, jnp.int32)
        _loop = jnp.arange(6250, dtype=jnp.int32)
        src = jnp.concatenate([_s, _d, _loop])
        dst = jnp.concatenate([_d, _s, _loop])
        _o = jnp.argsort(dst, stable=True)
        src = src[_o]
        dst = dst[_o]
        edge_type_8 = jax.random.randint(jax.random.fold_in(_gk, 13), (206250,), 0, 8, jnp.int32)
        edge_weight = jax.random.uniform(jax.random.fold_in(_gk, 14), (206250,), jnp.float32, 0.0, 1)
        return (x, src, dst, edge_type_8, edge_weight)
    x, src, dst, edge_type_8, edge_weight = _rec_inputs()

    def _L0_gnn_setup():
        import jax, jax.numpy as jnp
        import numpy as np
        N = 12500
        E = 200000
        DIM = 64
        HEADS = 4
        CH = DIM // HEADS
        NEG_SLOPE = 0.2
        LN_EPS = 1e-05
        key = jax.random.key(seed)
        ks = jax.random.split(key, 6)
        x = jax.random.normal(ks[0], (N, DIM), dtype=jnp.float32)
        edge_index = jax.random.randint(ks[1], (2, E), 0, N, dtype=jnp.int64)
        scale = 1.0 / np.sqrt(DIM)
        W = jax.random.normal(ks[2], (DIM, HEADS * CH), dtype=jnp.float32) * scale
        att_src = jax.random.normal(ks[3], (HEADS, CH), dtype=jnp.float32) * scale
        att_dst = jax.random.normal(ks[4], (HEADS, CH), dtype=jnp.float32) * scale
        bias = jnp.zeros((HEADS * CH,), dtype=jnp.float32)
        gamma = jnp.ones((DIM,), dtype=jnp.float32)
        beta = jnp.zeros((DIM,), dtype=jnp.float32)
        return dict(x=x, edge_index=edge_index, W=W, att_src=att_src, att_dst=att_dst, bias=bias, gamma=gamma, beta=beta)
    _L0_gnn_all = _L0_gnn_setup()
    _L0_gnn_in = {k: v for k, v in _L0_gnn_all.items() if k in ('W', 'att_src', 'att_dst', 'bias', 'gamma', 'beta')}
    del _L0_gnn_all

    def _L1_gnn_setup():
        import jax, jax.numpy as jnp
        import numpy as np
        N_NODES = 12500
        N_EDGES = 200000
        D_FEAT = 64
        D_OUT = 64
        key = jax.random.key(seed)
        k1, k2, k3, k4 = jax.random.split(key, 4)
        vertices = jax.random.normal(k1, (N_NODES, D_FEAT), dtype=jnp.float32)
        edges = jax.random.randint(k2, (2, N_EDGES), 0, N_NODES, dtype=jnp.int64)
        weight = jax.random.normal(k3, (D_OUT, D_FEAT), dtype=jnp.float32) * (1.0 / np.sqrt(D_FEAT))
        bias = jax.random.normal(k4, (D_OUT,), dtype=jnp.float32) * 0.01
        return {'vertices': vertices, 'edges': edges, 'weight': weight, 'bias': bias}
    _L1_gnn_all = _L1_gnn_setup()
    _L1_gnn_in = {k: v for k, v in _L1_gnn_all.items() if k in ('weight', 'bias')}
    del _L1_gnn_all

    def _L2_gnn_setup():
        import jax, jax.numpy as jnp
        import numpy as np
        N_NODES = 9375
        N_EDGES = 150000
        IN_DIM = 64
        OUT_DIM = 64
        key = jax.random.key(seed)
        k1, k2, k3, k4, k5, k6 = jax.random.split(key, 6)
        x = jax.random.normal(k1, (N_NODES, IN_DIM), dtype=jnp.float32)
        edge_weight = jax.random.uniform(k2, (N_EDGES,), dtype=jnp.float32)
        W = jax.random.normal(k3, (OUT_DIM, IN_DIM), dtype=jnp.float32) * (1.0 / np.sqrt(IN_DIM))
        b = jax.random.normal(k4, (OUT_DIM,), dtype=jnp.float32) * 0.01
        edge_src = jax.random.randint(k5, (N_EDGES,), 0, N_NODES, dtype=jnp.int32)
        edge_dst = jax.random.randint(k6, (N_EDGES,), 0, N_NODES, dtype=jnp.int32)
        return {'x': x, 'edge_weight': edge_weight, 'W': W, 'b': b, 'edge_src': edge_src, 'edge_dst': edge_dst}
    _L2_gnn_all = _L2_gnn_setup()
    _L2_gnn_in = {k: v for k, v in _L2_gnn_all.items() if k in ('W', 'b')}
    del _L2_gnn_all

    def _L3_gnn_setup():
        import jax, jax.numpy as jnp
        import numpy as np
        N_NODES = 6250
        N_EDGES = 100000
        D_IN, D_HID, D_OUT = (64, 64, 64)
        N_REL, N_BASES = (8, 4)

        def _per_edge_inv_deg(dst, edge_type, n_nodes, n_rel):
            deg = jnp.zeros((n_rel, n_nodes), jnp.float32).at[edge_type, dst].add(1.0)
            return 1.0 / jnp.maximum(deg[edge_type, dst], 1.0)

        def _rgcn_conv(x, src, dst, edge_type, inv_deg, basis, comp, root, bias):
            n_nodes = x.shape[0]
            xs = x[src]
            c = comp[edge_type]
            m = c[:, 0:1] * (xs @ basis[0])
            for b in range(1, basis.shape[0]):
                m = m + c[:, b:b + 1] * (xs @ basis[b])
            agg = jax.ops.segment_sum(m * inv_deg[:, None], dst, num_segments=n_nodes)
            return agg + x @ root + bias
        key = jax.random.key(seed)
        ks = jax.random.split(key, 12)
        x = jax.random.normal(ks[0], (N_NODES, D_IN), dtype=jnp.float32)
        src = jax.random.randint(ks[1], (N_EDGES,), 0, N_NODES)
        dst = jax.random.randint(ks[2], (N_EDGES,), 0, N_NODES)
        edge_index = jnp.stack([src, dst]).astype(jnp.int64)
        edge_type = jax.random.randint(ks[3], (N_EDGES,), 0, N_REL).astype(jnp.int64)
        s = 0.1
        return {'x': x, 'edge_index': edge_index, 'edge_type': edge_type, 'basis1': jax.random.normal(ks[4], (N_BASES, D_IN, D_HID), jnp.float32) * s, 'comp1': jax.random.normal(ks[5], (N_REL, N_BASES), jnp.float32) * s, 'root1': jax.random.normal(ks[6], (D_IN, D_HID), jnp.float32) * s, 'bias1': jnp.zeros((D_HID,), jnp.float32), 'basis2': jax.random.normal(ks[7], (N_BASES, D_HID, D_OUT), jnp.float32) * s, 'comp2': jax.random.normal(ks[8], (N_REL, N_BASES), jnp.float32) * s, 'root2': jax.random.normal(ks[9], (D_HID, D_OUT), jnp.float32) * s, 'bias2': jnp.zeros((D_OUT,), jnp.float32)}
    _L3_gnn_all = _L3_gnn_setup()
    _L3_gnn_in = {k: v for k, v in _L3_gnn_all.items() if k in ('basis1', 'comp1', 'root1', 'bias1', 'basis2', 'comp2', 'root2', 'bias2')}
    del _L3_gnn_all
    return {'x': x, 'src': src, 'dst': dst, 'edge_type_8': edge_type_8, 'edge_weight': edge_weight, 'L0_gnn_W': _L0_gnn_in['W'], 'L0_gnn_att_src': _L0_gnn_in['att_src'], 'L0_gnn_att_dst': _L0_gnn_in['att_dst'], 'L0_gnn_bias': _L0_gnn_in['bias'], 'L0_gnn_gamma': _L0_gnn_in['gamma'], 'L0_gnn_beta': _L0_gnn_in['beta'], 'L1_gnn_weight': _L1_gnn_in['weight'], 'L1_gnn_bias': _L1_gnn_in['bias'], 'L2_gnn_W': _L2_gnn_in['W'], 'L2_gnn_b': _L2_gnn_in['b'], 'L3_gnn_basis1': _L3_gnn_in['basis1'], 'L3_gnn_comp1': _L3_gnn_in['comp1'], 'L3_gnn_root1': _L3_gnn_in['root1'], 'L3_gnn_bias1': _L3_gnn_in['bias1'], 'L3_gnn_basis2': _L3_gnn_in['basis2'], 'L3_gnn_comp2': _L3_gnn_in['comp2'], 'L3_gnn_root2': _L3_gnn_in['root2'], 'L3_gnn_bias2': _L3_gnn_in['bias2']}

def reference(x, src, dst, edge_type_8, edge_weight, L0_gnn_W, L0_gnn_att_src, L0_gnn_att_dst, L0_gnn_bias, L0_gnn_gamma, L0_gnn_beta, L1_gnn_weight, L1_gnn_bias, L2_gnn_W, L2_gnn_b, L3_gnn_basis1, L3_gnn_comp1, L3_gnn_root1, L3_gnn_bias1, L3_gnn_basis2, L3_gnn_comp2, L3_gnn_root2, L3_gnn_bias2):
    import jax
    import jax.numpy as jnp

    def _L0_gnn_ref(x, edge_index, W, att_src, att_dst, bias, gamma, beta):
        import jax, jax.numpy as jnp
        import numpy as np
        N = 12500
        E = 200000
        DIM = 64
        HEADS = 4
        CH = DIM // HEADS
        NEG_SLOPE = 0.2
        LN_EPS = 1e-05
        n = x.shape[0]
        loops = jnp.arange(n, dtype=edge_index.dtype)
        src = jnp.concatenate([edge_index[0], loops])
        dst = jnp.concatenate([edge_index[1], loops])
        h = (x @ W).reshape(n, HEADS, CH)
        a_src = jnp.einsum('nhc,hc->nh', h, att_src)
        a_dst = jnp.einsum('nhc,hc->nh', h, att_dst)
        e = a_src[src] + a_dst[dst]
        e = jax.nn.leaky_relu(e, NEG_SLOPE)
        m = jax.ops.segment_max(e, dst, num_segments=n)
        e = jnp.exp(e - m[dst])
        s = jax.ops.segment_sum(e, dst, num_segments=n)
        alpha = e / (s[dst] + 1e-16)
        msg = h[src] * alpha[:, :, None]
        out = jax.ops.segment_sum(msg, dst, num_segments=n)
        out = out.reshape(n, HEADS * CH) + bias
        y = x + out
        mu = jnp.mean(y, axis=-1, keepdims=True)
        var = jnp.var(y, axis=-1, keepdims=True)
        return (y - mu) / jnp.sqrt(var + LN_EPS) * gamma + beta

    def _L1_gnn_ref(vertices, edges, weight, bias):
        import jax, jax.numpy as jnp
        import numpy as np
        N_NODES = 12500
        N_EDGES = 200000
        D_FEAT = 64
        D_OUT = 64
        n_vertices = vertices.shape[0]
        idx = jnp.arange(n_vertices, dtype=edges.dtype)
        dst = jnp.concatenate([edges[0], idx])
        src = jnp.concatenate([edges[1], idx])
        agg = jax.ops.segment_sum(vertices[src], dst, num_segments=n_vertices)
        deg = jax.ops.segment_sum(jnp.ones_like(dst, dtype=vertices.dtype), dst, num_segments=n_vertices)
        agg = agg * (jnp.clip(deg, 1.0, None) ** (-0.5))[:, None]
        return agg @ weight.T + bias

    def _L2_gnn_ref(x, edge_weight, W, b, edge_src, edge_dst):
        import jax, jax.numpy as jnp
        import numpy as np
        N_NODES = 9375
        N_EDGES = 150000
        IN_DIM = 64
        OUT_DIM = 64
        msgs = x[edge_src] * edge_weight[:, None]
        agg = jax.ops.segment_sum(msgs, edge_dst, num_segments=x.shape[0])
        return agg @ W.T + b

    def _L3_gnn_ref(x, edge_index, edge_type, basis1, comp1, root1, bias1, basis2, comp2, root2, bias2):
        import jax, jax.numpy as jnp
        import numpy as np
        N_NODES = 6250
        N_EDGES = 100000
        D_IN, D_HID, D_OUT = (64, 64, 64)
        N_REL, N_BASES = (8, 4)

        def _per_edge_inv_deg(dst, edge_type, n_nodes, n_rel):
            deg = jnp.zeros((n_rel, n_nodes), jnp.float32).at[edge_type, dst].add(1.0)
            return 1.0 / jnp.maximum(deg[edge_type, dst], 1.0)

        def _rgcn_conv(x, src, dst, edge_type, inv_deg, basis, comp, root, bias):
            n_nodes = x.shape[0]
            xs = x[src]
            c = comp[edge_type]
            m = c[:, 0:1] * (xs @ basis[0])
            for b in range(1, basis.shape[0]):
                m = m + c[:, b:b + 1] * (xs @ basis[b])
            agg = jax.ops.segment_sum(m * inv_deg[:, None], dst, num_segments=n_nodes)
            return agg + x @ root + bias
        src, dst = (edge_index[0], edge_index[1])
        inv_deg = _per_edge_inv_deg(dst, edge_type, x.shape[0], comp1.shape[0])
        h = _rgcn_conv(x, src, dst, edge_type, inv_deg, basis1, comp1, root1, bias1)
        h = jax.nn.relu(h)
        return _rgcn_conv(h, src, dst, edge_type, inv_deg, basis2, comp2, root2, bias2)
    edge_index = jnp.stack([src, dst])
    h = jnp.maximum(_layernorm(x, axis=-1), 0.0)
    x = x + _L0_gnn_ref(h, edge_index, L0_gnn_W, L0_gnn_att_src, L0_gnn_att_dst, L0_gnn_bias, L0_gnn_gamma, L0_gnn_beta)
    h = jnp.maximum(_layernorm(x, axis=-1), 0.0)
    x = x + _L1_gnn_ref(h, edge_index, L1_gnn_weight, L1_gnn_bias)
    h = jnp.maximum(_layernorm(x, axis=-1), 0.0)
    x = x + _L2_gnn_ref(h, edge_weight, L2_gnn_W, L2_gnn_b, src, dst)
    h = jnp.maximum(_layernorm(x, axis=-1), 0.0)
    x = x + _L3_gnn_ref(h, edge_index, edge_type_8, L3_gnn_basis1, L3_gnn_comp1, L3_gnn_root1, L3_gnn_bias1, L3_gnn_basis2, L3_gnn_comp2, L3_gnn_root2, L3_gnn_bias2)
    return x

_drawn_inputs = setup_inputs


def setup_inputs(seed=0):
    import zlib

    import numpy as np

    out = dict(_drawn_inputs(seed))
    spreads = {'L0_gnn_bias': (0.0, 0.1),
     'L0_gnn_gamma': (1.0, 0.2),
     'L0_gnn_beta': (0.0, 0.1),
     'L3_gnn_bias1': (0.0, 0.8),
     'L3_gnn_bias2': (0.0, 2.0)}
    factors = {'L0_gnn_att_dst': 23.013,
     'L1_gnn_bias': 8.0,
     'L2_gnn_b': 54.049,
     'L3_gnn_basis1': 3.805,
     'L3_gnn_comp1': 5.111,
     'L3_gnn_basis2': 5.169,
     'L3_gnn_comp2': 8.0}
    for name, (base, spread) in spreads.items():
        noise = np.random.default_rng([zlib.crc32(name.encode()), seed]).standard_normal(out[name].shape)
        drawn = base * np.exp(spread * noise) if base else spread * noise
        out[name] = jnp.asarray(drawn.astype(out[name].dtype))
    for name, factor in factors.items():
        out[name] = (out[name] * factor).astype(out[name].dtype)
    return out
```

```python
import concourse.bass as bass
from concourse import mybir
from contextlib import ExitStack

NODES = 6250
EDGES = 206250
DIM = 64
HEADS = 4
CH = DIM // HEADS
RELS = 8
BASES = 4
SLOPE = 0.2
EPS = 1e-5

P = 128
WINDOWS = -(-NODES // P)
TAIL = NODES - (WINDOWS - 1) * P
ROWS = WINDOWS * P
COLS = -(-EDGES // P)
LAST = EDGES - (COLS - 1) * P
K = 13
GROUPS = COLS // K
SLOTS = 4
ITERS = GROUPS // SLOTS
AHEAD = SLOTS * K
SPAN = 2
RUNS = -(-WINDOWS // SPAN)
WPAD = RUNS * SPAN
assert GROUPS * K == COLS and ITERS * SLOTS == GROUPS
PADNODE = 8191
WIDE = DIM + 8
CHUNK = 7
CHUNKS = WINDOWS // CHUNK
assert CHUNK * CHUNKS == WINDOWS
PAIRS = -(-K // 2)
BANKS = 4
BIG = 1e30
RANGE = 80.0


def gnn_stack(nc, x, src, dst, etype, eweight, w0, att_src, att_dst, bias0, gamma0, beta0, w1t, b1, w2t, b2,
              basis1, comp1, root1, bias1, basis2, comp2, root2, bias2, out):
    f32, i32, bf16 = mybir.dt.float32, mybir.dt.int32, mybir.dt.bfloat16
    ALU, ACT, AX = mybir.AluOpType, mybir.ActivationFunctionType, mybir.AxisListType

    t0 = nc.dram_tensor("rows_l0", (ROWS, DIM + HEADS), f32, kind="Internal").ap()
    t1 = nc.dram_tensor("rows_l1", (ROWS, DIM), f32, kind="Internal").ap()
    t2 = nc.dram_tensor("rows_l2", (ROWS, DIM), f32, kind="Internal").ap()
    t3 = nc.dram_tensor("rows_l3a", (ROWS * RELS, DIM), f32, kind="Internal").ap()
    t4 = nc.dram_tensor("rows_l3b", (ROWS * RELS, DIM), f32, kind="Internal").ap()

    ctx = ExitStack()
    with ctx:
        def sb(name, shape, dt=f32):
            return ctx.enter_context(nc.sbuf_tensor(name, shape, dt))

        def sem(name):
            return ctx.enter_context(nc.semaphore(name))

        X = sb("X", [P, WINDOWS, DIM])
        Hn = sb("Hn", [P, WINDOWS, DIM])
        Y = sb("Y", [P, WINDOWS, WIDE])
        acc = sb("acc", [P, WPAD, WIDE])
        tmp = sb("tmp", [P, WINDOWS, DIM])
        st = sb("st", [P, 3, WINDOWS])
        attn = sb("attn", [P, WPAD, 8])
        inv = sb("inv", [P, WPAD, RELS])
        ns = sb("ns", [P, 2, WPAD, HEADS])
        amax = sb("amax", [P, WPAD, HEADS])
        tab = sb("tab", [P, WPAD, 3, 8], bf16)
        tres = sb("tres", [P, WPAD, 8])
        srcF = sb("srcF", [P, COLS + AHEAD])
        relsrcF = sb("relsrcF", [P, COLS + AHEAD])
        typF = sb("typF", [P, COLS])
        ew = sb("ew", [P, COLS])
        rel0 = sb("rel0", [P, COLS])
        rel = sb("rel", [P, COLS])
        idx = sb("idx", [P, SLOTS, K], i32)
        G = sb("G", [P, SLOTS, K, WIDE])
        S = sb("S", [P, 2, K, SPAN * P])
        ST = sb("ST", [P, 2, K, SPAN * P], bf16)
        W = sb("W", [P, 2, K, DIM + HEADS])
        tabw = sb("tabw", [P, 2, SPAN, 24], bf16)
        f1 = sb("f1", [P, K, 8])
        f2 = sb("f2", [P, K, 8])
        sc = sb("sc", [P, K, 8])
        wt = sb("wt", [P, K])
        ident = sb("ident", [P, P])
        ones = sb("ones", [P, P])
        iota_i = sb("iota_i", [P, SPAN * P], i32)
        iota = sb("iota", [P, SPAN * P])
        epsc = sb("epsc", [P, 1])
        onec = sb("onec", [P, 1])
        rows = sb("rows", [P, 7, DIM])
        W0 = sb("W0", [DIM, WIDE])
        att = sb("att", [DIM, 2, DIM])
        attw = sb("attw", [DIM, 2, DIM])
        W1 = sb("W1", [DIM, DIM])
        W2 = sb("W2", [DIM, DIM])
        basis = sb("basis", [DIM, 2, BASES, DIM])
        comp = sb("comp", [DIM, 2, RELS, BASES])
        Wr = sb("Wr", [DIM, 2, RELS + 1, DIM])
        hT = sb("hT", [DIM, 2, CHUNK * P])
        wrow = sb("wrow", [1, 4, GROUPS])
        wint = sb("wint", [1, 2, GROUPS], i32)
        stat = sb("stat", [P, 9])
        stT = sb("stT", [9, P])
        stv = sb("stv", [9, 1])
        stD = sb("stD", [9, 9])
        stA = sb("stA", [P, 9])
        flag = sb("flag", [P, 8])
        runs_i = sb("runs_i", [1, 1], i32)

        dstI = S[:, 0, :, :].rearrange("p k j -> p (k j)")[:, 0:COLS].bitcast(i32)
        srcI = S[:, 0, :, :].rearrange("p k j -> p (k j)")[:, COLS:2 * COLS].bitcast(i32)
        typI = S[:, 1, :, :].rearrange("p k j -> p (k j)")[:, 0:COLS].bitcast(i32)
        dstF = S[:, 1, :, :].rearrange("p k j -> p (k j)")[:, COLS:2 * COLS]
        stage = S[:, :, :, :].rearrange("p a k j -> p (a k j)")[:, 0:BANKS * RELS * DIM]\
            .rearrange("p (b n) -> p b n", b=BANKS)

        ps = [ctx.enter_context(nc.psum_tensor(f"ps{i}", [P, 512], f32)) for i in range(8)]
        flip = ps[0:4]
        summed_ps = ps[4:6]
        fetch_ps = ps[6:8]

        s_load = sem("s_load")
        s_edges = sem("s_edges")
        s_x = sem("s_x")
        s_xtail = sem("s_xtail")
        s_wts = sem("s_wts")
        s_const = sem("s_const")
        s_pool = sem("s_pool")
        s_dve = sem("s_dve")
        s_var = sem("s_var")
        s_std = sem("s_std")
        s_h = sem("s_h")
        s_hT = sem("s_hT")
        s_hTc = sem("s_hTc")
        s_y = sem("s_y")
        s_yc = sem("s_yc")
        s_row = sem("s_row")
        s_rowb = sem("s_rowb")
        s_stat = sem("s_stat")
        s_statT = sem("s_statT")
        s_statD = sem("s_statD")
        s_statA = sem("s_statA")
        s_runs = sem("s_runs")
        s_maxed = sem("s_maxed")
        s_stc = [sem("s_stc_act"), sem("s_stc_dve")]
        s_rooted = sem("s_rooted")
        s_rootc = sem("s_rootc")
        s_table = [sem(f"s_table{n}") for n in range(5)]
        s_stage = [sem(f"s_stage{n}") for n in range(BANKS)]
        s_self = sem("s_self")
        s_pself = sem("s_pself")
        s_out = sem("s_out")

        class Pass:
            def __init__(self, n, kind, table, width, summed_width, order):
                self.n, self.kind, self.table, self.width = n, kind, table, width
                self.summed_width, self.order = summed_width, order
                self.fetches = kind in ("attention", "relation")
                self.begun = sem(f"p{n}_begun")
                self.idx_ready = sem(f"p{n}_idx_ready")
                self.gathered = [sem(f"p{n}_gathered{s}") for s in range(SLOTS)]
                self.gathering = sem(f"p{n}_gathering")
                self.onehot = sem(f"p{n}_onehot")
                self.flipped = sem(f"p{n}_flipped")
                self.flip_copied = sem(f"p{n}_flip_copied")
                self.fetched = sem(f"p{n}_fetched")
                self.exp_in = sem(f"p{n}_exp_in")
                self.exp_out = sem(f"p{n}_exp_out")
                self.weighted = sem(f"p{n}_weighted")
                self.summed = sem(f"p{n}_summed")
                self.step = sem(f"p{n}_step")

        passes = [
            Pass(0, "attention", t0, DIM + HEADS, DIM + HEADS, srcF),
            Pass(1, "count", t1, DIM, WIDE, srcF),
            Pass(2, "weight", t2, DIM, DIM, srcF),
            Pass(3, "relation", t3, DIM, DIM, relsrcF),
            Pass(4, "relation", t4, DIM, DIM, relsrcF),
        ]
        m_begun = sem("m_begun")
        m_idx = sem("m_idx")
        m_gathered = sem("m_gathered")
        m_ready = sem("m_ready")
        m_scored = sem("m_scored")
        m_taken = sem("m_taken")
        m_step = sem("m_step")

        block = ctx.enter_context(nc.Block())

        @block.sync
        def _(sp):
            sp.dma_start(dstI, dst).then_inc(s_edges, 16)
            sp.dma_start(srcI, src).then_inc(s_edges, 16)
            sp.dma_start(typI, etype).then_inc(s_edges, 16)
            sp.dma_start(ew[:, :], eweight).then_inc(s_edges, 16)
            sp.dma_start(X[:, 0:WINDOWS - 1, :],
                         x[0:(WINDOWS - 1) * P, :].rearrange("(w p) c -> p w c", p=P)).then_inc(s_x, 16)
            sp.wait_ge(s_xtail, 1)
            sp.dma_start(X[0:TAIL, WINDOWS - 1, :], x[(WINDOWS - 1) * P:NODES, :]).then_inc(s_x, 16)
            for n, width in ((0, DIM + HEADS), (1, DIM), (2, DIM)):
                tv = passes[n].table.rearrange("(w p) c -> p w c", p=P)
                for c in range(CHUNKS):
                    sp.wait_ge(s_yc, n * CHUNKS + c + 1)
                    sp.dma_start(tv[:, c * CHUNK:(c + 1) * CHUNK, :],
                                 Y[:, c * CHUNK:(c + 1) * CHUNK, 0:width]).then_inc(s_table[n], 16)
            for n in (3, 4):
                tv = passes[n].table.rearrange("(w p r) c -> w p (r c)", p=P, r=RELS)
                for w in range(WINDOWS):
                    v = (n - 3) * WINDOWS + w
                    sp.wait_ge(s_stc[w % 2], (n - 3) * ((WINDOWS + 1 - w % 2) // 2) + w // 2 + 1)
                    sp.dma_start(tv[w, :, :], stage[:, v % BANKS, :]).then_inc(s_stage[v % BANKS], 16)
            sp.wait_ge(s_out, 1)
            sp.dma_start(out[0:(WINDOWS - 1) * P, :].rearrange("(w p) c -> p w c", p=P),
                         X[:, 0:WINDOWS - 1, :]).then_inc(s_load, 16)
            sp.dma_start(out[(WINDOWS - 1) * P:NODES, :], X[0:TAIL, WINDOWS - 1, :]).then_inc(s_load, 16)
            sp.wait_ge(s_load, 32)
            for n in range(3):
                sp.wait_ge(s_table[n], 16 * CHUNKS)
            for b in range(BANKS):
                sp.wait_ge(s_stage[b], 16 * len(range(b, 2 * WINDOWS, BANKS)))

        @block.gpsimd
        def _(pool):
            pool.iota(iota_i[:, :], [[1, SPAN * P]], base=0, channel_multiplier=0).then_inc(s_const, 1)
            pool.memset(ident[:, :], 0.0).then_inc(s_pool, 1)
            pool.memset(ones[:, :], 1.0).then_inc(s_const, 1)
            pool.memset(epsc[:, :], EPS).then_inc(s_const, 1)
            pool.memset(onec[:, :], 1.0).then_inc(s_const, 1)
            pool.wait_ge(s_pool, 1)
            pool.affine_select(out=ident[:, :], in_=ident[:, :], compare_op=ALU.not_equal, fill=1.0,
                               base=0, pattern=[[-1, P]], channel_multiplier=1).then_inc(s_const, 1)
            pool.wait_ge(s_runs, 1)
            runs = pool.value_load(runs_i[0:1, 0:1], min_val=1, max_val=RUNS)

            pool.wait_ge(s_table[0], 16 * CHUNKS)
            with pool.If(runs > 1):
                with pool.Fori(0, RUNS) as r:
                    with pool.Fori(0, GROUPS) as g:
                        pool.wait_ge(m_idx, r * GROUPS + g + 1)
                        pool.sem_inc(m_begun, 1)
                        for k in range(K):
                            pool.indirect_dma_start(
                                G[:, 0, k, 0:DIM + HEADS], None, t0,
                                bass.IndirectOffsetOnAxis(ap=idx[:, 0, k:k + 1], axis=0)).then_inc(m_gathered, 16)

            for p in passes:
                if p.n < 3:
                    pool.wait_ge(s_table[p.n], 16 * CHUNKS)
                else:
                    for b in range(BANKS):
                        pool.wait_ge(s_stage[b], 16 * len(range(b, (p.n - 2) * WINDOWS, BANKS)))
                with pool.Fori(0, RUNS) as r:
                    with pool.If(r < runs):
                        with pool.Fori(0, ITERS) as i:
                            for s in range(SLOTS):
                                pool.wait_ge(p.idx_ready, r * (GROUPS + SLOTS) + i * SLOTS + s + 1)
                                pool.wait_ge(p.summed, r * GROUPS + i * SLOTS + s + 1)
                                pool.sem_inc(p.gathering, 1)
                                for k in range(K):
                                    pool.indirect_dma_start(
                                        G[:, s, k, 0:p.width], None, p.table,
                                        bass.IndirectOffsetOnAxis(ap=idx[:, s, k:k + 1], axis=0)
                                    ).then_inc(p.gathered[s], 16)

        @block.scalar
        def _(act):
            for n, v in enumerate((bias0, gamma0, beta0, b1, b2, bias1, bias2)):
                act.dma_start(rows[:, n, :], v.rearrange("(a c) -> a c", a=1).to_broadcast((P, DIM))).then_inc(s_wts, 16)
            for n, v in enumerate((att_src, att_dst)):
                act.dma_start(att[:, n, :], v.rearrange("h c -> (h c)").rearrange("(a c) -> a c", a=1)
                              .to_broadcast((DIM, DIM))).then_inc(s_wts, 16)
            act.dma_start(W0[:, 0:DIM], w0).then_inc(s_wts, 16)
            act.dma_start(W1[:, :], w1t).then_inc(s_wts, 16)
            act.dma_start(W2[:, :], w2t).then_inc(s_wts, 16)
            for n, (b, c, rt) in enumerate(((basis1, comp1, root1), (basis2, comp2, root2))):
                act.dma_start(basis[:, n, :, :], b.rearrange("b i o -> i b o")).then_inc(s_wts, 16)
                act.dma_start(comp[:, n, :, :].rearrange("p r b -> p (r b)"),
                              c.rearrange("r b -> (r b)").rearrange("(a c) -> a c", a=1)
                              .to_broadcast((DIM, RELS * BASES))).then_inc(s_wts, 16)
                act.dma_start(Wr[:, n, RELS, :], rt).then_inc(s_wts, 16)

            def std(n):
                act.wait_ge(s_var, n)
                act.activation(st[:, 2, :], st[:, 1, :], ACT.Sqrt, bias=epsc[:, 0:1], scale=1.0 / DIM).then_inc(s_std, 1)

            def copy_turned(n):
                for c in range(CHUNKS):
                    v = n * CHUNKS + c
                    act.wait_ge(s_hT, v + 1)
                    if v >= 2:
                        act.wait_ge(s_y, v - 1)
                    act.activation(hT[:, v % 2, 0:512], ps[0 + 2 * (v % 2)][0:DIM, :], ACT.Copy).then_inc(s_hTc, 1)
                    act.activation(hT[:, v % 2, 512:CHUNK * P], ps[1 + 2 * (v % 2)][0:DIM, 0:CHUNK * P - 512],
                                   ACT.Copy).then_inc(s_hTc, 1)
                    if n >= 3:
                        for j in range(CHUNK):
                            w = c * CHUNK + j
                            if w % 2 == 0:
                                stage_window(act, n, w)

            def stage_window(eng, n, w):
                u = (n - 3) * WINDOWS + w
                eng.wait_ge(s_rooted, u + 1)
                if u >= BANKS:
                    eng.wait_ge(s_stage[u % BANKS], 16 * (u // BANKS))
                eng.activation(stage[:, u % BANKS, :], ps[4 + w % 2][:, :], ACT.Copy).then_inc(s_stc[0], 1)

            act.wait_ge(s_const, 5)
            std(1)
            copy_turned(0)
            act.wait_ge(s_runs, 1)
            runs = act.value_load(runs_i[0:1, 0:1], min_val=1, max_val=RUNS)
            with act.If(runs > 1):
                act.sem_inc(m_taken, K)
                with act.Fori(0, RUNS) as r:
                    with act.Fori(0, GROUPS) as g:
                        act.wait_ge(m_taken, (r * GROUPS + g + 1) * K)
                        act.activation(idx[:, 0, :], srcF[:, bass.ds(g * K, K)], ACT.Copy).then_inc(m_idx, 1)

            for p in passes:
                act.wait_ge(p.begun, 1)
                if p.fetches:
                    act.sem_inc(p.flip_copied, BANKS)
                with act.Fori(0, RUNS) as r:
                    with act.If(r < runs):
                        for s in range(SLOTS):
                            if s == 0:
                                act.wait_ge(p.begun, r + 1)
                            act.activation(idx[:, s, :], p.order[:, s * K:(s + 1) * K], ACT.Copy).then_inc(p.idx_ready, 1)
                        with act.Fori(0, ITERS) as i:
                            for s in range(SLOTS):
                                n = r * GROUPS + i * SLOTS + s
                                if p.fetches:
                                    act.wait_ge(p.fetched, n + 1)
                                    for c in range(PAIRS):
                                        m = min(2, K - 2 * c)
                                        act.wait_ge(p.flipped, n * PAIRS + c + 1)
                                        act.activation(
                                            ST[:, s % 2, 2 * c:2 * c + m, :].rearrange("p k j -> p (k j)"),
                                            flip[(PAIRS * s + c) % BANKS][:, 0:m * SPAN * P],
                                            ACT.Copy).then_inc(p.flip_copied, 1)
                                act.wait_ge(p.gathered[s], (r * ITERS + i + 1) * (K * 16))
                                act.activation(idx[:, s, :], p.order[:, bass.ds((i * SLOTS + s + SLOTS) * K, K)],
                                               ACT.Copy).then_inc(p.idx_ready, 1)
                                if p.kind == "attention":
                                    act.wait_ge(p.exp_in, n + 1)
                                    act.activation(W[:, s % 2, :, DIM:DIM + HEADS], sc[:, :, 0:HEADS],
                                                   ACT.Exp).then_inc(p.exp_out, 1)
                if p.kind == "attention":
                    act.wait_ge(s_self, 1)
                    act.activation(ns[:, 1, 0:WINDOWS, :], ns[:, 0, 0:WINDOWS, :], ACT.Exp).then_inc(s_pself, 1)
                    std(2)
                    std(3)
                if p.kind == "count":
                    act.wait_ge(s_self, 2)
                    act.activation(st[:, 1, :], st[:, 0, :], ACT.Sqrt).then_inc(s_pself, 1)
                    std(4)
                if p.kind == "weight":
                    std(5)
                if p.n < 4:
                    copy_turned(p.n + 1)

        @block.tensor
        def _(pe):
            def turn(n):
                pe.wait_ge(s_h, n + 1)
                rhs = (W0[:, 0:WIDE], W1[:, :], W2[:, :], None, None)[n]
                width = WIDE if n == 0 else DIM

                def flips(c):
                    v = n * CHUNKS + c
                    if v >= 2:
                        pe.wait_ge(s_hTc, 2 * (v - 1))
                    for j in range(CHUNK):
                        last = pe.transpose(ps[j // 4 + 2 * (v % 2)][0:DIM, (j % 4) * P:(j % 4 + 1) * P],
                                            Hn[:, c * CHUNK + j, :], ident[:, :])
                    last.then_inc(s_hT, 1)

                flips(0)
                for c in range(CHUNKS):
                    v = n * CHUNKS + c
                    if c + 1 < CHUNKS:
                        flips(c + 1)
                    pe.wait_ge(s_hTc, 2 * (v + 1))
                    if v >= 2:
                        pe.wait_ge(s_yc, v - 1)
                    for j in range(CHUNK):
                        w = c * CHUNK + j
                        if n < 3:
                            last = pe.matmul(ps[6 + v % 2][:, j * WIDE:j * WIDE + width],
                                             hT[:, v % 2, j * P:(j + 1) * P], rhs, start=True, stop=True)
                        else:
                            u = (n - 3) * WINDOWS + w
                            if w >= 2:
                                pe.wait_ge(s_stc[w % 2], (n - 3) * ((WINDOWS + 1 - w % 2) // 2) + w // 2)
                            pe.matmul(ps[4 + w % 2][:, :], hT[:, v % 2, j * P:(j + 1) * P],
                                      Wr[:, n - 3, 0:RELS, :].rearrange("i r o -> i (r o)"),
                                      start=True, stop=True).then_inc(s_rooted, 1)
                            last = pe.matmul(ps[6 + v % 2][:, j * WIDE:j * WIDE + DIM],
                                             hT[:, v % 2, j * P:(j + 1) * P], Wr[:, n - 3, RELS, :],
                                             start=True, stop=True)
                    last.then_inc(s_y, 1)

            pe.wait_ge(s_const, 5)
            pe.wait_ge(s_row, 1)
            pe.matmul(ps[7][:, 0:GROUPS], ones[0:1, :], wrow[0:1, 2, :], start=True, stop=True).then_inc(s_rowb, 1)
            turn(0)
            pe.wait_ge(s_stat, 1)
            pe.transpose(ps[4][0:9, 0:P], stat[:, :], ident[:, :]).then_inc(s_statT, 1)
            pe.wait_ge(s_statD, 1)
            pe.matmul(ps[5][:, 0:9], ones[0:9, :], stD[:, :], start=True, stop=True).then_inc(s_statA, 1)
            pe.wait_ge(s_row, 2)
            pe.matmul(ps[7][:, 0:GROUPS], ones[0:1, :], wrow[0:1, 2, :], start=True, stop=True).then_inc(s_rowb, 1)
            pe.wait_ge(s_runs, 1)
            runs = pe.value_load(runs_i[0:1, 0:1], min_val=1, max_val=RUNS)

            with pe.If(runs > 1):
                with pe.Fori(0, RUNS) as r:
                    with pe.Fori(0, GROUPS) as g:
                        for k in range(K):
                            pe.wait_ge(m_ready, (r * GROUPS + g) * K + k + 1)
                            for q in range(SPAN):
                                pe.matmul(ps[q][:, :], S[:, 0, 0, q * P:(q + 1) * P],
                                          S[:, 0, 2:4, :].rearrange("p a j -> p (a j)"), start=True, stop=False)
                                last = pe.matmul(ps[q][:, :], S[:, 0, 1, q * P:(q + 1) * P],
                                                 S[:, 0, 4:6, :].rearrange("p a j -> p (a j)"), start=False, stop=True)
                            last.then_inc(m_scored, 1)

            for p in passes:
                pe.wait_ge(p.begun, 1)
                pe.sem_inc(p.summed, SLOTS)
                if p.fetches:
                    pe.sem_inc(p.fetched, 2)

                with pe.Fori(0, RUNS) as r:
                    with pe.If(r < runs):
                        with pe.Fori(0, ITERS) as i:
                            def fetch(s):
                                n = r * GROUPS + i * SLOTS + s
                                pe.wait_ge(p.onehot, n + 1)
                                for c in range(PAIRS):
                                    pe.wait_ge(p.flip_copied, n * PAIRS + c + 1)
                                    m = min(2, K - 2 * c)
                                    for h in range(m):
                                        for q in range(SPAN):
                                            at = (h * SPAN + q) * P
                                            last = pe.transpose(flip[(PAIRS * s + c) % BANKS][:, at:at + P],
                                                                S[:, s % 2, 2 * c + h, q * P:(q + 1) * P], ident[:, :])
                                    last.then_inc(p.flipped, 1)
                                pe.wait_ge(p.flip_copied, n * PAIRS + PAIRS + BANKS)
                                for k in range(K):
                                    for q in range(SPAN):
                                        last = pe.matmul(fetch_ps[s % 2][:, k * 24:(k + 1) * 24],
                                                         ST[:, s % 2, k, q * P:(q + 1) * P], tabw[:, s % 2, q, :],
                                                         start=(q == 0), stop=(q == SPAN - 1))
                                last.then_inc(p.fetched, 1)

                            def sums(s):
                                n = r * GROUPS + i * SLOTS + s
                                pe.wait_ge(p.weighted, n + 1)
                                if p.kind == "count":
                                    pe.wait_ge(p.gathered[s], (r * ITERS + i + 1) * (K * 16))
                                for q in range(SPAN):
                                    for k in range(K):
                                        rhs = G[:, s, k, :] if p.kind == "count" else W[:, s % 2, k, 0:p.summed_width]
                                        last = pe.matmul(
                                            summed_ps[s % 2][:, q * WIDE:q * WIDE + p.summed_width],
                                            S[:, s % 2, k, q * P:(q + 1) * P], rhs,
                                            start=(k == 0), stop=(k == K - 1))
                                last.then_inc(p.summed, 1)

                            if p.fetches:
                                fetch(0)
                            for s in range(SLOTS):
                                if s < SLOTS - 1 and p.fetches:
                                    fetch(s + 1)
                                sums(s)
                if p.n < 4:
                    turn(p.n + 1)

        @block.vector
        def _(dve):
            done = [0]

            def link(ins):
                done[0] += 1
                ins.then_inc(s_dve, 1)
                dve.wait_ge(s_dve, done[0])

            def bc(a, n):
                return a[:, :, None].to_broadcast((*a.shape, n)) if len(a.shape) == 2 else \
                    a[:, :, :, None].to_broadcast((*a.shape, n))

            def along(n, m=WINDOWS):
                return rows[:, n, :][:, None, :].to_broadcast((P, m, DIM))

            wide = acc[:, 0:WINDOWS, 0:DIM]
            stds = [0]

            def center(v):
                stds[0] += 1
                link(dve.tensor_reduce(st[:, 0, :], v, AX.X, ALU.add))
                link(dve.tensor_scalar(st[:, 0, :], st[:, 0, :], 1.0 / DIM, None, ALU.mult))
                link(dve.tensor_tensor(tmp[:, :, :], v, bc(st[:, 0, :], DIM), ALU.subtract))
                link(dve.tensor_tensor(wide, tmp[:, :, :], tmp[:, :, :], ALU.mult))
                dve.tensor_reduce(st[:, 1, :], wide, AX.X, ALU.add).then_inc(s_var, 1)
                dve.wait_ge(s_std, stds[0])
                link(dve.reciprocal(st[:, 2, :], st[:, 2, :]))

            def norm_relu():
                center(X[:, :, :])
                dve.scalar_tensor_tensor(out=Hn[:, :, :], in0=tmp[:, :, :], scalar=0.0, in1=bc(st[:, 2, :], DIM),
                                         op0=ALU.max, op1=ALU.mult).then_inc(s_h, 1)

            def copy_y(n):
                width = WIDE if n == 0 else DIM
                for c in range(CHUNKS):
                    v = n * CHUNKS + c
                    if n >= 3:
                        for j in range(CHUNK):
                            w = c * CHUNK + j
                            if w % 2 == 1:
                                u = (n - 3) * WINDOWS + w
                                dve.wait_ge(s_rooted, u + 1)
                                if u >= BANKS:
                                    dve.wait_ge(s_stage[u % BANKS], 16 * (u // BANKS))
                                dve.tensor_copy(stage[:, u % BANKS, :], ps[4 + w % 2][:, :]).then_inc(s_stc[1], 1)
                    dve.wait_ge(s_y, v + 1)
                    dve.tensor_copy(Y[:, c * CHUNK:(c + 1) * CHUNK, 0:width],
                                    ps[6 + v % 2][:, 0:CHUNK * WIDE].rearrange("p (w c) -> p w c", c=WIDE)[:, :, 0:width]
                                    ).then_inc(s_yc, 1)

            def split(v):
                link(dve.tensor_copy(tab[:, :, 0, :], v))
                link(dve.tensor_tensor(tres[:, :, :], v, tab[:, :, 0, :], ALU.subtract))
                link(dve.tensor_copy(tab[:, :, 1, :], tres[:, :, :]))
                link(dve.tensor_tensor(tab[:, :, 2, :], tres[:, :, :], tab[:, :, 1, :], ALU.subtract))

            def windows_for(eff):
                return eff

            link(dve.memset(X[:, WINDOWS - 1, :], 0.0))
            dve.memset(srcF[:, COLS:], 0.0)
            dve.memset(relsrcF[:, COLS:], 0.0)
            dve.memset(acc[:, WINDOWS:, :], 0.0)
            dve.memset(attn[:, WINDOWS:, :], 0.0)
            link(dve.memset(amax[:, WINDOWS:, :], 0.0))
            dve.sem_inc(s_xtail, 1)
            dve.wait_ge(s_const, 5)
            dve.wait_ge(s_edges, 64)
            dve.tensor_copy(iota[:, :], iota_i[:, :])
            dve.tensor_copy(srcF[:, 0:COLS], srcI)
            dve.tensor_copy(typF[:, :], typI)
            link(dve.tensor_copy(dstF, dstI))
            dve.scalar_tensor_tensor(out=relsrcF[:, 0:COLS], in0=srcF[:, 0:COLS], scalar=float(RELS),
                                     in1=typF[:, :], op0=ALU.mult, op1=ALU.add)
            first = dstI[0:1, 0:COLS].rearrange("p (g k) -> p g k", k=K)[:, :, 0]
            link(dve.tensor_scalar(wint[0:1, 0, :], first, 7, None, ALU.arith_shift_right))
            link(dve.tensor_copy(wrow[0:1, 0, :], wint[0:1, 0, :]))
            link(dve.tensor_scalar(wrow[0:1, 1, :], wrow[0:1, 0, :], float(WINDOWS - SPAN), 0.0, ALU.min, ALU.max))
            link(dve.tensor_scalar(wrow[0:1, 2, :], wrow[0:1, 1, :], float(P), None, ALU.mult))
            dve.sem_inc(s_row, 1)

            def relative():
                link(dve.tensor_tensor(rel0[:, :].rearrange("p (g k) -> p g k", k=K),
                                       dstF.rearrange("p (g k) -> p g k", k=K),
                                       bc(ps[7][:, 0:GROUPS], K), ALU.subtract))

            dve.wait_ge(s_rowb, 1)
            relative()
            link(dve.tensor_scalar(rel[:, :], rel0[:, :], -(SPAN * P - 1) / 2.0, None, ALU.add))
            link(dve.tensor_tensor(rel[:, :], rel[:, :], rel[:, :], ALU.mult))
            link(dve.tensor_reduce(stat[:, 0:1], rel[:, 0:COLS - 1], AX.X, ALU.max))
            link(dve.tensor_tensor(stat[0:LAST, 0:1], stat[0:LAST, 0:1], rel[0:LAST, COLS - 1:COLS], ALU.max))

            dve.wait_ge(s_wts, 16 * 18)
            for n in range(2):
                for b in range(BASES):
                    bs = basis[:, n, b, :][:, None, :].to_broadcast((DIM, RELS, DIM))
                    cb = comp[:, n, :, b][:, :, None].to_broadcast((DIM, RELS, DIM))
                    d = Wr[:, n, 0:RELS, :]
                    t = tmp[0:DIM, 0:RELS, :]
                    if b == 0:
                        link(dve.tensor_tensor(d, bs, cb, ALU.mult))
                    else:
                        link(dve.tensor_tensor(t, bs, cb, ALU.mult))
                        link(dve.tensor_tensor(d, d, t, ALU.add))
            for n in range(2):
                link(dve.tensor_tensor(attw[:, n, :], att[:, n, :], W0[:, 0:DIM], ALU.mult))
                link(dve.tensor_reduce(W0[:, DIM + n * HEADS:DIM + (n + 1) * HEADS],
                                       attw[:, n, :].rearrange("p (h c) -> p h c", h=HEADS), AX.X, ALU.add))

            dve.wait_ge(s_x, 32)
            norm_relu()
            copy_y(0)
            dve.wait_ge(s_yc, CHUNKS)
            a_src, a_dst = Y[:, :, DIM:DIM + HEADS], Y[:, :, DIM + HEADS:WIDE]
            link(dve.tensor_reduce(stat[:, 1:5], a_src.rearrange("p w h -> p h w"), AX.X, ALU.max))
            link(dve.tensor_reduce(stat[:, 5:9], a_src.rearrange("p w h -> p h w"), AX.X, ALU.min))
            link(dve.tensor_scalar(stat[:, 5:9], stat[:, 5:9], -1.0, None, ALU.mult))
            dve.sem_inc(s_stat, 1)
            dve.wait_ge(s_statT, 1)
            link(dve.tensor_reduce(stv[:, :], ps[4][0:9, 0:P], AX.X, ALU.max))
            link(dve.tensor_scalar(stD[:, :], ident[0:9, 0:9], stv[:, 0:1], None, ALU.mult))
            dve.sem_inc(s_statD, 1)
            dve.wait_ge(s_statA, 1)
            link(dve.tensor_copy(stA[:, :], ps[5][:, 0:9]))
            link(dve.tensor_tensor(flag[:, 0:4], stA[:, 1:5], stA[:, 5:9], ALU.add))
            link(dve.tensor_reduce(flag[:, 4:5], flag[:, 0:4], AX.X, ALU.max))
            link(dve.tensor_scalar(flag[:, 5:6], flag[:, 4:5], RANGE, None, ALU.is_gt))
            link(dve.tensor_scalar(flag[:, 6:7], stA[:, 0:1], ((SPAN * P - 1) / 2.0) ** 2 + 1.0, None, ALU.is_gt))
            link(dve.tensor_tensor(flag[:, 7:8], flag[:, 5:6], flag[:, 6:7], ALU.max))
            link(dve.tensor_scalar(runs_i[0:1, :], flag[0:1, 7:8], float(RUNS - 1), 1.0, ALU.mult, ALU.add))
            link(dve.tensor_scalar(flag[0:1, 0:1], flag[0:1, 7:8], -1.0, 1.0, ALU.mult, ALU.add))
            link(dve.tensor_scalar(wrow[0:1, 1, :], wrow[0:1, 1, :], flag[0:1, 0:1], None, ALU.mult))
            link(dve.tensor_copy(wint[0:1, 0, :], wrow[0:1, 1, :]))
            link(dve.tensor_scalar(wrow[0:1, 2, :], wrow[0:1, 1, :], float(P), None, ALU.mult))
            dve.sem_inc(s_row, 1)
            dve.wait_ge(s_rowb, 2)
            relative()
            link(dve.tensor_copy(amax[:, 0:WINDOWS, :], stA[:, 1:5][:, None, :].to_broadcast((P, WINDOWS, HEADS))))
            dve.sem_inc(s_runs, 1)
            runs = dve.value_load(runs_i[0:1, 0:1], min_val=1, max_val=RUNS)

            def start_windows():
                dve.tensor_copy(rel[:, :], rel0[:, :])
                link(dve.tensor_copy(wint[0:1, 1, :], wint[0:1, 0, :]))

            start_windows()
            with dve.If(runs > 1):
                mine = [0]

                def mlink(ins, at):
                    mine[0] += 1
                    ins.then_inc(m_step, 1)
                    dve.wait_ge(m_step, at + mine[0])

                Sf, Sn = S[:, 0, 0, :], S[:, 0, 1, :]
                Dg = S[:, 0, 2:4, :].rearrange("p a j -> p (a j)").rearrange("p (h e) -> p h e", h=HEADS)
                Ii = S[:, 0, 4:6, :].rearrange("p a j -> p (a j)").rearrange("p (h e) -> p h e", h=HEADS)
                four = ident[:, None, :].to_broadcast((P, HEADS, P))
                mlink(dve.tensor_copy(Ii, four), 0)
                mlink(dve.tensor_copy(amax[:, 0:WINDOWS, :], a_src), 0)
                before = mine[0]
                STEPS = K * (2 + 2 * SPAN)
                with dve.Fori(0, RUNS) as r:
                    with dve.Fori(0, GROUPS) as g:
                        n = r * GROUPS + g
                        dve.wait_ge(m_gathered, (n + 1) * (K * 16))
                        w = dve.value_load(wint[0:1, 1, bass.ds(g, 1)], min_val=0, max_val=WPAD - SPAN)
                        mine[0] = before
                        at = n * STEPS + r * 2
                        for k in range(K):
                            mlink(dve.tensor_scalar(Sf, iota[:, :], rel[:, bass.ds(g * K + k, 1)], None,
                                                    ALU.is_equal), at)
                            dve.tensor_tensor(Dg, four, bc(G[:, 0, k, DIM:DIM + HEADS], P), ALU.mult)
                            mlink(dve.tensor_scalar(Sn, Sf, -1.0, BIG, ALU.add, ALU.mult), at)
                            dve.sem_inc(m_ready, 1)
                            dve.wait_ge(m_scored, n * K + k + 1)
                            for q in range(SPAN):
                                mlink(dve.tensor_reduce(sc[:, 0, 0:HEADS],
                                                        ps[q][:, :].rearrange("p (h e) -> p h e", h=HEADS),
                                                        AX.X, ALU.max), at)
                                to = amax[:, bass.ds(w + q, 1), :].rearrange("p a h -> p (a h)")
                                mlink(dve.tensor_tensor(to, to, sc[:, 0, 0:HEADS], ALU.max), at)
                            dve.sem_inc(m_taken, 1)
                    mine[0] = before
                    at = (r + 1) * (GROUPS * STEPS) + r * 2
                    mlink(dve.tensor_scalar(rel[:, :], rel[:, :], -float(SPAN * P), None, ALU.add), at)
                    mlink(dve.tensor_scalar(wint[0:1, 1, :], wint[0:1, 1, :], SPAN, None, ALU.add), at)
                    dve.sem_inc(s_maxed, 1)

            link(dve.tensor_copy(attn[:, 0:WINDOWS, 0:HEADS], a_dst))
            link(dve.tensor_tensor(ns[:, 0, 0:WINDOWS, :], amax[:, 0:WINDOWS, :], a_dst, ALU.add))
            link(dve.scalar_tensor_tensor(out=attn[:, 0:WINDOWS, HEADS:8], in0=ns[:, 0, 0:WINDOWS, :], scalar=SLOPE,
                                          in1=ns[:, 0, 0:WINDOWS, :], op0=ALU.mult, op1=ALU.max))
            split(attn[:, :, :])

            def edge_pass(p):
                link(dve.memset(acc[:, :, :], 0.0))
                start_windows()
                dve.sem_inc(p.begun, 1)
                with dve.Fori(0, RUNS) as r:
                    with dve.If(r < runs):
                        with dve.Fori(0, ITERS) as i:
                            steps = [0]

                            def plink(ins):
                                steps[0] += 1
                                ins.then_inc(p.step, 1)
                                dve.wait_ge(p.step, (r * ITERS + i) * PER_ITER + r * 2 + steps[0])

                            def num(s):
                                return r * GROUPS + i * SLOTS + s

                            def one_hot(s):
                                cols = bass.ds((i * SLOTS + s) * K, K)
                                if p.fetches:
                                    dve.tensor_copy(tabw[:, s % 2, :, :],
                                                    tab[:, bass.ds(ws[s], SPAN), :, :].rearrange("p w a c -> p w (a c)"))
                                if p.kind == "count":
                                    dve.tensor_tensor(G[:, s, :, DIM:WIDE],
                                                      iota[:, 0:RELS][:, None, :].to_broadcast((P, K, RELS)),
                                                      bc(typF[:, cols], RELS), ALU.is_equal)
                                ins = dve.tensor_tensor(S[:, s % 2, :, :],
                                                        iota[:, None, :].to_broadcast((P, K, SPAN * P)),
                                                        bc(rel[:, cols], SPAN * P), ALU.is_equal)
                                ins.then_inc(p.onehot, 1)

                            def weigh(s):
                                cols = bass.ds((i * SLOTS + s) * K, K)
                                if p.kind == "count":
                                    dve.wait_ge(p.onehot, num(s) + 1)
                                    dve.sem_inc(p.weighted, 1)
                                    return
                                if p.fetches:
                                    dve.wait_ge(p.fetched, num(s) + 1 + 2)
                                    three = fetch_ps[s % 2][:, 0:24 * K].rearrange("p (k a c) -> p k a c", k=K, a=3)
                                    plink(dve.tensor_copy(f1[:, :, :], three[:, :, 2, :]))
                                    plink(dve.tensor_tensor(f2[:, :, :], f1[:, :, :], three[:, :, 1, :], ALU.add))
                                    plink(dve.tensor_tensor(f1[:, :, :], f2[:, :, :], three[:, :, 0, :], ALU.add))
                                if p.kind == "relation":
                                    plink(dve.tensor_tensor(sc[:, :, :],
                                                            iota[:, 0:RELS][:, None, :].to_broadcast((P, K, RELS)),
                                                            bc(typF[:, cols], RELS), ALU.is_equal))
                                    plink(dve.tensor_tensor(sc[:, :, :], sc[:, :, :], f1[:, :, :], ALU.mult))
                                    plink(dve.tensor_reduce(wt[:, :], sc[:, :, :], AX.X, ALU.add))
                                dve.wait_ge(p.gathered[s], (r * ITERS + i + 1) * (K * 16))
                                if p.kind == "attention":
                                    plink(dve.tensor_tensor(sc[:, :, 0:HEADS], G[:, s, :, DIM:DIM + HEADS],
                                                            f1[:, :, 0:HEADS], ALU.add))
                                    plink(dve.scalar_tensor_tensor(out=sc[:, :, HEADS:8], in0=sc[:, :, 0:HEADS],
                                                                   scalar=SLOPE, in1=sc[:, :, 0:HEADS],
                                                                   op0=ALU.mult, op1=ALU.max))
                                    plink(dve.tensor_tensor(sc[:, :, 0:HEADS], sc[:, :, HEADS:8],
                                                            f1[:, :, HEADS:8], ALU.subtract))
                                    dve.sem_inc(p.exp_in, 1)
                                    dve.wait_ge(p.exp_out, num(s) + 1)
                                    dve.tensor_tensor(
                                        W[:, s % 2, :, 0:DIM].rearrange("p k (h c) -> p k h c", h=HEADS),
                                        G[:, s, :, 0:DIM].rearrange("p k (h c) -> p k h c", h=HEADS),
                                        bc(W[:, s % 2, :, DIM:DIM + HEADS], CH), ALU.mult).then_inc(p.weighted, 1)
                                else:
                                    weight = wt[:, :] if p.kind == "relation" else ew[:, cols]
                                    dve.tensor_tensor(W[:, s % 2, :, 0:DIM], G[:, s, :, 0:DIM],
                                                      bc(weight, DIM), ALU.mult).then_inc(p.weighted, 1)

                            def add(s):
                                dve.wait_ge(p.summed, num(s) + 1 + SLOTS)
                                to = acc[:, bass.ds(ws[s], SPAN), 0:p.summed_width]
                                part = summed_ps[s % 2][:, 0:SPAN * WIDE].rearrange("p (q c) -> p q c", q=SPAN)
                                plink(dve.tensor_tensor(to, to, part[:, :, 0:p.summed_width], ALU.add))

                            PER_ITER = SLOTS * (1 + {"attention": 6, "relation": 6, "count": 0, "weight": 0}[p.kind])
                            ws = [dve.value_load(wint[0:1, 1, bass.ds(i * SLOTS + s, 1)], min_val=0,
                                                 max_val=WPAD - SPAN) for s in range(SLOTS)]
                            one_hot(0)
                            for s in range(SLOTS):
                                if s > 0:
                                    add(s - 1)
                                if s < SLOTS - 1:
                                    one_hot(s + 1)
                                weigh(s)
                            add(SLOTS - 1)
                            assert steps[0] == PER_ITER
                        dve.tensor_scalar(rel[:, :], rel[:, :], -float(SPAN * P), None, ALU.add).then_inc(p.step, 1)
                        dve.tensor_scalar(wint[0:1, 1, :], wint[0:1, 1, :], SPAN, None, ALU.add).then_inc(p.step, 1)
                        dve.wait_ge(p.step, (r + 1) * (ITERS * PER_ITER) + (r + 1) * 2)
                        dve.sem_inc(p.begun, 1)

            edge_pass(passes[0])
            link(dve.tensor_tensor(ns[:, 0, 0:WINDOWS, :], a_src, a_dst, ALU.add))
            link(dve.scalar_tensor_tensor(out=ns[:, 1, 0:WINDOWS, :], in0=ns[:, 0, 0:WINDOWS, :], scalar=SLOPE,
                                          in1=ns[:, 0, 0:WINDOWS, :], op0=ALU.mult, op1=ALU.max))
            link(dve.tensor_tensor(ns[:, 0, 0:WINDOWS, :], ns[:, 1, 0:WINDOWS, :], attn[:, 0:WINDOWS, HEADS:8],
                                   ALU.subtract))
            dve.sem_inc(s_self, 1)
            dve.wait_ge(s_pself, 1)
            pself = ns[:, 1, 0:WINDOWS, :]
            t4d = tmp[:, :, :].rearrange("p w (h c) -> p w h c", h=HEADS)
            dve.tensor_tensor(t4d, Y[:, :, 0:DIM].rearrange("p w (h c) -> p w h c", h=HEADS), bc(pself, CH), ALU.mult)
            link(dve.tensor_tensor(acc[:, 0:WINDOWS, DIM:DIM + HEADS], acc[:, 0:WINDOWS, DIM:DIM + HEADS], pself, ALU.add))
            link(dve.tensor_tensor(wide, wide, tmp[:, :, :], ALU.add))
            link(dve.reciprocal(ns[:, 0, 0:WINDOWS, :], acc[:, 0:WINDOWS, DIM:DIM + HEADS]))
            w4d = wide.rearrange("p w (h c) -> p w h c", h=HEADS)
            link(dve.tensor_tensor(t4d, w4d, bc(ns[:, 0, 0:WINDOWS, :], CH), ALU.mult))
            link(dve.tensor_tensor(tmp[:, :, :], tmp[:, :, :], along(0), ALU.add))
            link(dve.tensor_tensor(Hn[:, :, :], Hn[:, :, :], tmp[:, :, :], ALU.add))
            center(Hn[:, :, :])
            link(dve.tensor_tensor(tmp[:, :, :], tmp[:, :, :], bc(st[:, 2, :], DIM), ALU.mult))
            link(dve.tensor_tensor(tmp[:, :, :], tmp[:, :, :], along(1), ALU.mult))
            link(dve.tensor_tensor(tmp[:, :, :], tmp[:, :, :], along(2), ALU.add))
            link(dve.tensor_tensor(X[:, :, :], X[:, :, :], tmp[:, :, :], ALU.add))

            norm_relu()
            copy_y(1)
            dve.wait_ge(s_yc, 2 * CHUNKS)
            edge_pass(passes[1])
            counts = acc[:, :, DIM:WIDE]
            link(dve.tensor_reduce(st[:, 2, :], acc[:, 0:WINDOWS, DIM:WIDE], AX.X, ALU.add))
            link(dve.tensor_scalar(st[:, 0, :], st[:, 2, :], 1.0, 1.0, ALU.add, ALU.max))
            dve.sem_inc(s_self, 1)
            link(dve.tensor_scalar(inv[:, :, :], counts, 1.0, None, ALU.max))
            link(dve.reciprocal(inv[:, :, :], inv[:, :, :]))
            split(inv[:, :, :])
            dve.wait_ge(s_pself, 2)
            link(dve.reciprocal(st[:, 0, :], st[:, 1, :]))
            link(dve.tensor_tensor(tmp[:, :, :], wide, Y[:, :, 0:DIM], ALU.add))
            link(dve.tensor_tensor(tmp[:, :, :], tmp[:, :, :], bc(st[:, 0, :], DIM), ALU.mult))
            link(dve.tensor_tensor(tmp[:, :, :], tmp[:, :, :], along(3), ALU.add))
            link(dve.tensor_tensor(X[:, :, :], X[:, :, :], tmp[:, :, :], ALU.add))

            norm_relu()
            copy_y(2)
            dve.wait_ge(s_yc, 3 * CHUNKS)
            edge_pass(passes[2])
            link(dve.tensor_tensor(tmp[:, :, :], wide, along(4), ALU.add))
            link(dve.tensor_tensor(X[:, :, :], X[:, :, :], tmp[:, :, :], ALU.add))

            norm_relu()
            copy_y(3)
            dve.wait_ge(s_yc, 4 * CHUNKS)
            for b in range(BANKS):
                dve.wait_ge(s_stage[b], 16 * len(range(b, WINDOWS, BANKS)))
            edge_pass(passes[3])
            link(dve.tensor_tensor(tmp[:, :, :], wide, Y[:, :, 0:DIM], ALU.add))
            link(dve.tensor_tensor(tmp[:, :, :], tmp[:, :, :], along(5), ALU.add))
            dve.tensor_scalar(Hn[:, :, :], tmp[:, :, :], 0.0, None, ALU.max).then_inc(s_h, 1)
            copy_y(4)
            dve.wait_ge(s_yc, 5 * CHUNKS)
            for b in range(BANKS):
                dve.wait_ge(s_stage[b], 16 * len(range(b, 2 * WINDOWS, BANKS)))
            edge_pass(passes[4])
            link(dve.tensor_tensor(tmp[:, :, :], wide, Y[:, :, 0:DIM], ALU.add))
            link(dve.tensor_tensor(tmp[:, :, :], tmp[:, :, :], along(6), ALU.add))
            link(dve.tensor_tensor(X[:, :, :], X[:, :, :], tmp[:, :, :], ALU.add))
            dve.sem_inc(s_out, 1)


_INS = ['x', 'src', 'dst', 'edge_type_8', 'edge_weight', 'L0_gnn_W', 'L0_gnn_att_src', 'L0_gnn_att_dst',
        'L0_gnn_bias', 'L0_gnn_gamma', 'L0_gnn_beta', 'L1_gnn_weight', 'L1_gnn_bias', 'L2_gnn_W', 'L2_gnn_b',
        'L3_gnn_basis1', 'L3_gnn_comp1', 'L3_gnn_root1', 'L3_gnn_bias1', 'L3_gnn_basis2', 'L3_gnn_comp2',
        'L3_gnn_root2', 'L3_gnn_bias2']


def kernel(**inputs):
    import numpy as _np
    import concourse.bacc as _bacc
    from concourse import mybir as _mybir
    from concourse.bass_utils import run_bass_kernel_spmd as _run

    def by_column(a, fill):
        full = _np.full(COLS * P, fill, a.dtype)
        full[:EDGES] = a
        return full.reshape(COLS, P).T

    nc = _bacc.Bacc("TRN2", target_bir_lowering=False, num_devices=1)
    arrays, args = {}, []
    for name in _INS:
        a = _np.asarray(inputs[name])
        if name in ("src", "edge_type_8", "edge_weight"):
            a = by_column(a, 0)
        if name == "dst":
            a = by_column(a, PADNODE)
        if name in ("L1_gnn_weight", "L2_gnn_W"):
            a = a.T
        a = _np.ascontiguousarray(a)
        arrays[f"in_{name}"] = a
        args.append(nc.dram_tensor(f"in_{name}", a.shape, _mybir.dt.from_np(a.dtype), kind="ExternalInput").ap())
    args.append(nc.dram_tensor("out_x", (NODES, DIM), _mybir.dt.float32, kind="ExternalOutput").ap())
    gnn_stack(nc, *args)
    r = _run(nc, [arrays], core_ids=[0])
    return r.results[0]["out_x"]
```

```python
import concourse.bass as bass
from concourse import mybir
from contextlib import ExitStack

NODES = 6250
EDGES = 206250
DIM = 64
HEADS = 4
CH = DIM // HEADS
RELS = 8
BASES = 4
SLOPE = 0.2
EPS = 1e-5

P = 128
WINDOWS = -(-NODES // P)
TAIL = NODES - (WINDOWS - 1) * P
ROWS = WINDOWS * P
COLS = -(-EDGES // P)
LAST = EDGES - (COLS - 1) * P
K = 13
GROUPS = COLS // K
SLOTS = 4
ITERS = GROUPS // SLOTS
AHEAD = SLOTS * K
SPAN = 2
RUNS = -(-WINDOWS // SPAN)
WPAD = RUNS * SPAN
assert GROUPS * K == COLS and ITERS * SLOTS == GROUPS
PADNODE = 8191
WIDE = DIM + 8
CHUNK = 7
CHUNKS = WINDOWS // CHUNK
assert CHUNK * CHUNKS == WINDOWS
BANKS = 4
FLIPS = -(-K // 4)
PARTS = 3
assert FLIPS == BANKS
BIG = 1e30
RANGE = 80.0


def gnn_stack(nc, x, src, dst, etype, eweight, w0, att_src, att_dst, bias0, gamma0, beta0, w1t, b1, w2t, b2,
              basis1, comp1, root1, bias1, basis2, comp2, root2, bias2, out):
    f32, i32, bf16 = mybir.dt.float32, mybir.dt.int32, mybir.dt.bfloat16
    ALU, ACT, AX = mybir.AluOpType, mybir.ActivationFunctionType, mybir.AxisListType

    t0 = nc.dram_tensor("rows_l0", (ROWS, DIM + HEADS), f32, kind="Internal").ap()
    t1 = nc.dram_tensor("rows_l1", (ROWS, PARTS * DIM), bf16, kind="Internal").ap()
    t2 = nc.dram_tensor("rows_l2", (ROWS, DIM), f32, kind="Internal").ap()
    t3 = nc.dram_tensor("rows_l3a", (ROWS * RELS, DIM), f32, kind="Internal").ap()
    t4 = nc.dram_tensor("rows_l3b", (ROWS * RELS, DIM), f32, kind="Internal").ap()

    ctx = ExitStack()
    with ctx:
        def sb(name, shape, dt=f32):
            return ctx.enter_context(nc.sbuf_tensor(name, shape, dt))

        def sem(name):
            return ctx.enter_context(nc.semaphore(name))

        X = sb("X", [P, WINDOWS, DIM])
        Hn = sb("Hn", [P, WINDOWS, DIM])
        Y = sb("Y", [P, WINDOWS, WIDE])
        acc = sb("acc", [P, WPAD, WIDE])
        tmp = sb("tmp", [P, WINDOWS, DIM])
        st = sb("st", [P, 3, WINDOWS])
        attn = sb("attn", [P, WPAD, 8])
        inv = sb("inv", [P, WPAD, RELS])
        ns = sb("ns", [P, 2, WPAD, HEADS])
        amax = sb("amax", [P, WPAD, HEADS])
        tab = sb("tab", [P, WPAD, 3, 8], bf16)
        tres = sb("tres", [P, WPAD, 8])
        srcF = sb("srcF", [P, COLS + AHEAD])
        relsrcF = sb("relsrcF", [P, COLS + AHEAD])
        typF = sb("typF", [P, COLS])
        ew = sb("ew", [P, COLS])
        rel0 = sb("rel0", [P, COLS + K])
        rel = sb("rel", [P, COLS + K])
        idx = sb("idx", [P, SLOTS, K], i32)
        G = sb("G", [P, SLOTS, K, (PARTS * DIM + RELS) // 2])
        Gb = G[:, :, :, :].bitcast(bf16)
        onehots = sb("onehots", [P, (SLOTS + 2) * K * SPAN * P], bf16)
        S = onehots[:, 0:SLOTS * K * SPAN * P].rearrange("p (a k j) -> p a k j", a=SLOTS, k=K)
        ST = onehots[:, SLOTS * K * SPAN * P:].rearrange("p (a k j) -> p a k j", a=2, k=K)
        before_rings = onehots[:, :].bitcast(f32)
        Wf = sb("Wf", [P, K, DIM + HEADS])
        Rf = sb("Rf", [P, K, DIM + HEADS])
        W3 = sb("W3", [P, 2, K, PARTS * (DIM + HEADS)], bf16)
        relw = sb("relw", [P, SLOTS, K])
        part = sb("part", [P, SPAN, DIM + HEADS])
        tabw = sb("tabw", [P, 2, SPAN, 24], bf16)
        f1 = sb("f1", [P, K, 8])
        f2 = sb("f2", [P, K, 8])
        sc = sb("sc", [P, K, 8])
        wt = sb("wt", [P, K])
        ident = sb("ident", [P, P])
        identb = sb("identb", [P, P], bf16)
        ones = sb("ones", [P, P])
        iota_i = sb("iota_i", [P, SPAN * P], i32)
        iota = sb("iota", [P, SPAN * P])
        iotab = sb("iotab", [P, SPAN * P], bf16)
        epsc = sb("epsc", [P, 1])
        onec = sb("onec", [P, 1])
        rows = sb("rows", [P, 7, DIM])
        W0 = sb("W0", [DIM, WIDE])
        W1 = sb("W1", [DIM, DIM])
        W2 = sb("W2", [DIM, DIM])
        at_first = acc[0:DIM, :, :].rearrange("p w c -> p (w c)")
        basis = at_first[:, 0:2 * BASES * DIM].rearrange("p (n b o) -> p n b o", n=2, b=BASES)
        comp = at_first[:, 512:512 + 2 * RELS * BASES].rearrange("p (n r b) -> p n r b", n=2, r=RELS)
        att = at_first[:, 640:640 + 2 * DIM].rearrange("p (n c) -> p n c", n=2)
        attw = at_first[:, 768:768 + 2 * DIM].rearrange("p (n c) -> p n c", n=2)
        Wr = sb("Wr", [DIM, 2, RELS + 1, DIM])
        wrow = sb("wrow", [1, 4, GROUPS])
        wint = sb("wint", [1, 2, GROUPS + 1], i32)
        stat = sb("stat", [P, 9])
        stT = sb("stT", [9, P])
        stv = sb("stv", [9, 1])
        stD = sb("stD", [9, 9])
        stA = sb("stA", [P, 9])
        flag = sb("flag", [P, 8])
        runs_i = sb("runs_i", [1, 1], i32)

        dstI, srcI, typI, dstF = (before_rings[:, n * COLS:(n + 1) * COLS] for n in range(4))
        dstI, srcI, typI = (v.bitcast(i32) for v in (dstI, srcI, typI))
        stage = before_rings[:, 0:BANKS * RELS * DIM].rearrange("p (b n) -> p b n", b=BANKS)
        hT = before_rings[0:DIM, (SLOTS + 2) * K * P - 2 * CHUNK * P:(SLOTS + 2) * K * P].rearrange("p (a n) -> p a n", a=2)
        rows3 = onehots[:, 0:WINDOWS * PARTS * DIM].rearrange("p (w a c) -> p w a c", w=WINDOWS, a=PARTS)

        ps = [ctx.enter_context(nc.psum_tensor(f"ps{i}", [P, 512], f32)) for i in range(8)]
        flip = ps[0:4]
        flipb = [b[:, :].bitcast(bf16) for b in flip]
        summed_ps = ps[4:6]
        fetch_ps = ps[6:8]

        s_load = sem("s_load")
        s_edges = sem("s_edges")
        s_x = sem("s_x")
        s_xtail = sem("s_xtail")
        s_wts = sem("s_wts")
        s_const = sem("s_const")
        s_pool = sem("s_pool")
        s_dve = sem("s_dve")
        s_var = sem("s_var")
        s_std = sem("s_std")
        s_h = sem("s_h")
        s_hT = sem("s_hT")
        s_hTc = sem("s_hTc")
        s_y = sem("s_y")
        s_yc = sem("s_yc")
        s_row = sem("s_row")
        s_rowb = sem("s_rowb")
        s_stat = sem("s_stat")
        s_statT = sem("s_statT")
        s_statD = sem("s_statD")
        s_statA = sem("s_statA")
        s_runs = sem("s_runs")
        s_maxed = sem("s_maxed")
        s_stc = [sem("s_stc_act"), sem("s_stc_dve")]
        s_rooted = sem("s_rooted")
        s_rows3 = sem("s_rows3")
        s_rootc = sem("s_rootc")
        s_table = [sem(f"s_table{n}") for n in range(5)]
        s_stage = [sem(f"s_stage{n}") for n in range(BANKS)]
        s_self = sem("s_self")
        s_pself = sem("s_pself")
        s_out = sem("s_out")

        class Pass:
            def __init__(self, n, kind, table, width, summed_width, order):
                self.n, self.kind, self.table, self.width = n, kind, table, width
                self.summed_width, self.order = summed_width, order
                self.fetches = kind in ("attention", "relation")
                self.begun = sem(f"p{n}_begun")
                self.idx_ready = sem(f"p{n}_idx_ready")
                self.gathered = [sem(f"p{n}_gathered{s}") for s in range(SLOTS)]
                self.gathering = sem(f"p{n}_gathering")
                self.onehot = sem(f"p{n}_onehot")
                self.flipped = sem(f"p{n}_flipped")
                self.flip_copied = sem(f"p{n}_flip_copied")
                self.fetched = sem(f"p{n}_fetched")
                self.exp_in = sem(f"p{n}_exp_in")
                self.exp_out = sem(f"p{n}_exp_out")
                self.whole = sem(f"p{n}_whole")
                self.high = sem(f"p{n}_high")
                self.rest = sem(f"p{n}_rest")
                self.middle = sem(f"p{n}_middle")
                self.weighted = sem(f"p{n}_weighted")
                self.summed = sem(f"p{n}_summed")
                self.step = sem(f"p{n}_step")

        passes = [
            Pass(0, "attention", t0, DIM + HEADS, DIM + HEADS, srcF),
            Pass(1, "count", t1, DIM, WIDE, srcF),
            Pass(2, "weight", t2, DIM, DIM, srcF),
            Pass(3, "relation", t3, DIM, DIM, relsrcF),
            Pass(4, "relation", t4, DIM, DIM, relsrcF),
        ]
        m_begun = sem("m_begun")
        m_idx = sem("m_idx")
        m_gathered = sem("m_gathered")
        m_ready = sem("m_ready")
        m_scored = sem("m_scored")
        m_taken = sem("m_taken")
        m_step = sem("m_step")

        block = ctx.enter_context(nc.Block())

        @block.sync
        def _(sp):
            sp.dma_start(dstI, dst).then_inc(s_edges, 16)
            sp.dma_start(srcI, src).then_inc(s_edges, 16)
            sp.dma_start(typI, etype).then_inc(s_edges, 16)
            sp.dma_start(ew[:, :], eweight).then_inc(s_edges, 16)
            sp.dma_start(X[:, 0:WINDOWS - 1, :],
                         x[0:(WINDOWS - 1) * P, :].rearrange("(w p) c -> p w c", p=P)).then_inc(s_x, 16)
            sp.wait_ge(s_xtail, 1)
            sp.dma_start(X[0:TAIL, WINDOWS - 1, :], x[(WINDOWS - 1) * P:NODES, :]).then_inc(s_x, 16)
            for n in range(3):
                tv = passes[n].table.rearrange("(w p) c -> p w c", p=P)
                for c in range(CHUNKS):
                    ws = slice(c * CHUNK, (c + 1) * CHUNK)
                    if n == 1:
                        sp.wait_ge(s_rows3, c + 1)
                        rows_of = rows3[:, ws, :, :].rearrange("p w a c -> p w (a c)")
                    else:
                        sp.wait_ge(s_yc, n * CHUNKS + c + 1)
                        rows_of = Y[:, ws, 0:passes[n].width]
                    sp.dma_start(tv[:, ws, :], rows_of).then_inc(s_table[n], 16)
            for n in (3, 4):
                tv = passes[n].table.rearrange("(w p r) c -> w p (r c)", p=P, r=RELS)
                for w in range(WINDOWS):
                    v = (n - 3) * WINDOWS + w
                    sp.wait_ge(s_stc[w % 2], (n - 3) * ((WINDOWS + 1 - w % 2) // 2) + w // 2 + 1)
                    sp.dma_start(tv[w, :, :], stage[:, v % BANKS, :]).then_inc(s_stage[v % BANKS], 16)
            sp.wait_ge(s_out, 1)
            sp.dma_start(out[0:(WINDOWS - 1) * P, :].rearrange("(w p) c -> p w c", p=P),
                         X[:, 0:WINDOWS - 1, :]).then_inc(s_load, 16)
            sp.dma_start(out[(WINDOWS - 1) * P:NODES, :], X[0:TAIL, WINDOWS - 1, :]).then_inc(s_load, 16)
            sp.wait_ge(s_load, 32)
            for n in range(3):
                sp.wait_ge(s_table[n], 16 * CHUNKS)
            for b in range(BANKS):
                sp.wait_ge(s_stage[b], 16 * len(range(b, 2 * WINDOWS, BANKS)))

        @block.gpsimd
        def _(pool):
            pool.iota(iota_i[:, :], [[1, SPAN * P]], base=0, channel_multiplier=0).then_inc(s_const, 1)
            pool.memset(ident[:, :], 0.0).then_inc(s_pool, 1)
            pool.memset(ones[:, :], 1.0).then_inc(s_const, 1)
            pool.memset(epsc[:, :], EPS).then_inc(s_const, 1)
            pool.memset(onec[:, :], 1.0).then_inc(s_const, 1)
            pool.memset(identb[:, :], 0.0).then_inc(s_pool, 1)
            pool.wait_ge(s_pool, 2)
            for m in (ident, identb):
                pool.affine_select(out=m[:, :], in_=m[:, :], compare_op=ALU.not_equal, fill=1.0,
                                   base=0, pattern=[[-1, P]], channel_multiplier=1).then_inc(s_const, 1)
            pool.wait_ge(s_runs, 1)
            runs = pool.value_load(runs_i[0:1, 0:1], min_val=1, max_val=RUNS)

            pool.wait_ge(s_table[0], 16 * CHUNKS)
            with pool.If(runs > 1):
                with pool.Fori(0, RUNS) as r:
                    with pool.Fori(0, GROUPS) as g:
                        pool.wait_ge(m_idx, r * GROUPS + g + 1)
                        pool.sem_inc(m_begun, 1)
                        for k in range(K):
                            pool.indirect_dma_start(
                                G[:, 0, k, 0:DIM + HEADS], None, t0,
                                bass.IndirectOffsetOnAxis(ap=idx[:, 0, k:k + 1], axis=0)).then_inc(m_gathered, 16)

            for p in passes:
                if p.n < 3:
                    pool.wait_ge(s_table[p.n], 16 * CHUNKS)
                else:
                    for b in range(BANKS):
                        pool.wait_ge(s_stage[b], 16 * len(range(b, (p.n - 2) * WINDOWS, BANKS)))
                with pool.Fori(0, RUNS) as r:
                    with pool.If(r < runs):
                        with pool.Fori(0, ITERS) as i:
                            for s in range(SLOTS):
                                pool.wait_ge(p.idx_ready, r * (GROUPS + SLOTS) + i * SLOTS + s + 1)
                                pool.wait_ge(p.summed, r * GROUPS + i * SLOTS + s + 1)
                                pool.sem_inc(p.gathering, 1)
                                for k in range(K):
                                    row = Gb[:, s, k, 0:PARTS * DIM] if p.kind == "count" else G[:, s, k, 0:p.width]
                                    pool.indirect_dma_start(
                                        row, None, p.table,
                                        bass.IndirectOffsetOnAxis(ap=idx[:, s, k:k + 1], axis=0)
                                    ).then_inc(p.gathered[s], 16)

        @block.scalar
        def _(act):
            for n, v in enumerate((bias0, gamma0, beta0, b1, b2, bias1, bias2)):
                act.dma_start(rows[:, n, :], v.rearrange("(a c) -> a c", a=1).to_broadcast((P, DIM))).then_inc(s_wts, 16)
            for n, v in enumerate((att_src, att_dst)):
                act.dma_start(att[:, n, :], v.rearrange("h c -> (h c)").rearrange("(a c) -> a c", a=1)
                              .to_broadcast((DIM, DIM))).then_inc(s_wts, 16)
            act.dma_start(W0[:, 0:DIM], w0).then_inc(s_wts, 16)
            act.dma_start(W1[:, :], w1t).then_inc(s_wts, 16)
            act.dma_start(W2[:, :], w2t).then_inc(s_wts, 16)
            for n, (b, c, rt) in enumerate(((basis1, comp1, root1), (basis2, comp2, root2))):
                act.dma_start(basis[:, n, :, :], b.rearrange("b i o -> i b o")).then_inc(s_wts, 16)
                act.dma_start(comp[:, n, :, :].rearrange("p r b -> p (r b)"),
                              c.rearrange("r b -> (r b)").rearrange("(a c) -> a c", a=1)
                              .to_broadcast((DIM, RELS * BASES))).then_inc(s_wts, 16)
                act.dma_start(Wr[:, n, RELS, :], rt).then_inc(s_wts, 16)

            def std(n):
                act.wait_ge(s_var, n)
                act.activation(st[:, 2, :], st[:, 1, :], ACT.Sqrt, bias=epsc[:, 0:1], scale=1.0 / DIM).then_inc(s_std, 1)

            def copy_turned(n):
                for c in range(CHUNKS):
                    v = n * CHUNKS + c
                    act.wait_ge(s_hT, v + 1)
                    if v >= 2:
                        act.wait_ge(s_y, v - 1)
                    act.activation(hT[:, v % 2, 0:512], ps[0 + 2 * (v % 2)][0:DIM, :], ACT.Copy).then_inc(s_hTc, 1)
                    act.activation(hT[:, v % 2, 512:CHUNK * P], ps[1 + 2 * (v % 2)][0:DIM, 0:CHUNK * P - 512],
                                   ACT.Copy).then_inc(s_hTc, 1)
                    if n >= 3:
                        for j in range(CHUNK):
                            w = c * CHUNK + j
                            if w % 2 == 0:
                                stage_window(act, n, w)

            def stage_window(eng, n, w):
                u = (n - 3) * WINDOWS + w
                eng.wait_ge(s_rooted, u + 1)
                if u >= BANKS:
                    eng.wait_ge(s_stage[u % BANKS], 16 * (u // BANKS))
                eng.activation(stage[:, u % BANKS, :], ps[4 + w % 2][:, :], ACT.Copy).then_inc(s_stc[0], 1)

            act.wait_ge(s_const, 6)
            std(1)
            copy_turned(0)
            act.wait_ge(s_runs, 1)
            runs = act.value_load(runs_i[0:1, 0:1], min_val=1, max_val=RUNS)
            with act.If(runs > 1):
                act.sem_inc(m_taken, K)
                with act.Fori(0, RUNS) as r:
                    with act.Fori(0, GROUPS) as g:
                        act.wait_ge(m_taken, (r * GROUPS + g + 1) * K)
                        act.activation(idx[:, 0, :], srcF[:, bass.ds(g * K, K)], ACT.Copy).then_inc(m_idx, 1)

            for p in passes:
                act.wait_ge(p.begun, 1)
                if p.fetches:
                    act.sem_inc(p.flip_copied, BANKS)
                with act.Fori(0, RUNS) as r:
                    with act.If(r < runs):
                        for s in range(SLOTS):
                            if s == 0:
                                act.wait_ge(p.begun, r + 1)
                            act.activation(idx[:, s, :], p.order[:, s * K:(s + 1) * K], ACT.Copy).then_inc(p.idx_ready, 1)
                        def copy_flips(chunks, at, s):
                            for c in chunks:
                                m = min(4, K - 4 * c)
                                act.wait_ge(p.flipped, at * FLIPS + c + 1)
                                act.activation(ST[:, s % 2, 4 * c:4 * c + m, :].rearrange("p k j -> p (k j)"),
                                               flipb[c][:, 0:m * SPAN * P], ACT.Copy).then_inc(p.flip_copied, 1)

                        if p.fetches:
                            act.wait_ge(p.fetched, r * (GROUPS + 1) + 1)
                            copy_flips(range(FLIPS), r * (GROUPS + 1), 0)
                        with act.Fori(0, ITERS) as i:
                            for s in range(SLOTS):
                                n = r * GROUPS + i * SLOTS + s
                                ahead = r * (GROUPS + 1) + i * SLOTS + s + 1
                                if p.fetches:
                                    act.wait_ge(p.fetched, ahead + 1)
                                    copy_flips((0,), ahead, s + 1)
                                act.wait_ge(p.gathered[s], (r * ITERS + i + 1) * (K * 16))
                                act.activation(idx[:, s, :], p.order[:, bass.ds((i * SLOTS + s + SLOTS) * K, K)],
                                               ACT.Copy).then_inc(p.idx_ready, 1)
                                if p.kind == "attention":
                                    act.wait_ge(p.exp_in, n + 1)
                                    act.activation(Wf[:, :, DIM:DIM + HEADS], sc[:, :, 0:HEADS],
                                                   ACT.Exp).then_inc(p.exp_out, 1)
                                if p.fetches:
                                    copy_flips((1,), ahead, s + 1)
                                if p.kind == "count":
                                    continue
                                v = p.width
                                act.wait_ge(p.whole, n + 1)
                                act.activation(W3[:, s % 2, :, 0:v], Wf[:, :, 0:v], ACT.Copy).then_inc(p.high, 1)
                                if p.fetches:
                                    copy_flips((2,), ahead, s + 1)
                                act.wait_ge(p.rest, n + 1)
                                act.activation(W3[:, s % 2, :, v:2 * v], Rf[:, :, 0:v], ACT.Copy).then_inc(p.middle, 1)
                                if p.fetches:
                                    copy_flips((3,), ahead, s + 1)
                if p.kind == "attention":
                    act.wait_ge(s_self, 1)
                    act.activation(ns[:, 1, 0:WINDOWS, :], ns[:, 0, 0:WINDOWS, :], ACT.Exp).then_inc(s_pself, 1)
                    std(2)
                    std(3)
                if p.kind == "count":
                    act.wait_ge(s_self, 2)
                    act.activation(st[:, 1, :], st[:, 0, :], ACT.Sqrt).then_inc(s_pself, 1)
                    std(4)
                if p.kind == "weight":
                    std(5)
                if p.n < 4:
                    copy_turned(p.n + 1)

        @block.tensor
        def _(pe):
            def turn(n):
                pe.wait_ge(s_h, n + 1)
                rhs = (W0[:, 0:WIDE], W1[:, :], W2[:, :], None, None)[n]
                width = WIDE if n == 0 else DIM

                def flips(c):
                    v = n * CHUNKS + c
                    if v >= 2:
                        pe.wait_ge(s_hTc, 2 * (v - 1))
                    for j in range(CHUNK):
                        last = pe.transpose(ps[j // 4 + 2 * (v % 2)][0:DIM, (j % 4) * P:(j % 4 + 1) * P],
                                            Hn[:, c * CHUNK + j, :], ident[:, :])
                    last.then_inc(s_hT, 1)

                flips(0)
                for c in range(CHUNKS):
                    v = n * CHUNKS + c
                    if c + 1 < CHUNKS:
                        flips(c + 1)
                    pe.wait_ge(s_hTc, 2 * (v + 1))
                    if v >= 2:
                        pe.wait_ge(s_yc, v - 1)
                    for j in range(CHUNK):
                        w = c * CHUNK + j
                        if n < 3:
                            last = pe.matmul(ps[6 + v % 2][:, j * WIDE:j * WIDE + width],
                                             hT[:, v % 2, j * P:(j + 1) * P], rhs, start=True, stop=True)
                        else:
                            u = (n - 3) * WINDOWS + w
                            if w >= 2:
                                pe.wait_ge(s_stc[w % 2], (n - 3) * ((WINDOWS + 1 - w % 2) // 2) + w // 2)
                            pe.matmul(ps[4 + w % 2][:, :], hT[:, v % 2, j * P:(j + 1) * P],
                                      Wr[:, n - 3, 0:RELS, :].rearrange("i r o -> i (r o)"),
                                      start=True, stop=True).then_inc(s_rooted, 1)
                            last = pe.matmul(ps[6 + v % 2][:, j * WIDE:j * WIDE + DIM],
                                             hT[:, v % 2, j * P:(j + 1) * P], Wr[:, n - 3, RELS, :],
                                             start=True, stop=True)
                    last.then_inc(s_y, 1)

            pe.wait_ge(s_const, 6)
            pe.wait_ge(s_row, 1)
            pe.matmul(ps[7][:, 0:GROUPS], ones[0:1, :], wrow[0:1, 2, :], start=True, stop=True).then_inc(s_rowb, 1)
            turn(0)
            pe.wait_ge(s_stat, 1)
            pe.transpose(ps[4][0:9, 0:P], stat[:, :], ident[:, :]).then_inc(s_statT, 1)
            pe.wait_ge(s_statD, 1)
            pe.matmul(ps[5][:, 0:9], ones[0:9, :], stD[:, :], start=True, stop=True).then_inc(s_statA, 1)
            pe.wait_ge(s_row, 2)
            pe.matmul(ps[7][:, 0:GROUPS], ones[0:1, :], wrow[0:1, 2, :], start=True, stop=True).then_inc(s_rowb, 1)
            pe.wait_ge(s_runs, 1)
            runs = pe.value_load(runs_i[0:1, 0:1], min_val=1, max_val=RUNS)

            with pe.If(runs > 1):
                with pe.Fori(0, RUNS) as r:
                    with pe.Fori(0, GROUPS) as g:
                        for k in range(K):
                            pe.wait_ge(m_ready, (r * GROUPS + g) * K + k + 1)
                            for q in range(SPAN):
                                pe.matmul(ps[q][:, :], before_rings[:, q * P:(q + 1) * P],
                                          before_rings[:, 512:1024], start=True, stop=False)
                                last = pe.matmul(ps[q][:, :], before_rings[:, 256 + q * P:256 + (q + 1) * P],
                                                 before_rings[:, 1024:1536], start=False, stop=True)
                            last.then_inc(m_scored, 1)

            for p in passes:
                pe.wait_ge(p.begun, 1)
                pe.sem_inc(p.summed, SLOTS)
                if p.fetches:
                    pe.sem_inc(p.fetched, 2)

                with pe.Fori(0, RUNS) as r:
                    with pe.If(r < runs):
                        def fetch(at, s):
                            pe.wait_ge(p.onehot, at + 1)
                            for c in range(FLIPS):
                                pe.wait_ge(p.flip_copied, at * FLIPS + c + 1)
                                for h in range(min(4, K - 4 * c)):
                                    for q in range(SPAN):
                                        to = (h * SPAN + q) * P
                                        last = pe.transpose(flipb[c][:, to:to + P],
                                                            S[:, s % SLOTS, 4 * c + h, q * P:(q + 1) * P], identb[:, :])
                                last.then_inc(p.flipped, 1)
                            pe.wait_ge(p.flip_copied, (at + 1) * FLIPS + BANKS)
                            for k in range(K):
                                for q in range(SPAN):
                                    last = pe.matmul(fetch_ps[s % 2][:, k * 24:(k + 1) * 24],
                                                     ST[:, s % 2, k, q * P:(q + 1) * P], tabw[:, s % 2, q, :],
                                                     start=(q == 0), stop=(q == SPAN - 1))
                            last.then_inc(p.fetched, 1)

                        def sums(at, i, s):
                            if p.kind == "count":
                                pe.wait_ge(p.gathered[s], (r * ITERS + i + 1) * (K * 16))
                            pe.wait_ge(p.weighted, at + 1)
                            v = PARTS * p.width + (RELS if p.kind == "count" else 0)
                            for q in range(SPAN):
                                for k in range(K):
                                    rhs = Gb[:, s, k, 0:v] if p.kind == "count" else W3[:, s % 2, k, 0:v]
                                    last = pe.matmul(summed_ps[s % 2][:, q * 204:q * 204 + v],
                                                     S[:, s % SLOTS, k, q * P:(q + 1) * P], rhs,
                                                     start=(k == 0), stop=(k == K - 1))
                            last.then_inc(p.summed, 1)

                        if p.fetches:
                            fetch(r * (GROUPS + 1), 0)
                        with pe.Fori(0, ITERS) as i:
                            for s in range(SLOTS):
                                if p.fetches:
                                    fetch(r * (GROUPS + 1) + i * SLOTS + s + 1, s + 1)
                                sums(r * GROUPS + i * SLOTS + s, i, s)
                if p.n < 4:
                    turn(p.n + 1)

        @block.vector
        def _(dve):
            done = [0]

            def link(ins):
                done[0] += 1
                ins.then_inc(s_dve, 1)
                dve.wait_ge(s_dve, done[0])

            def bc(a, n):
                return a[:, :, None].to_broadcast((*a.shape, n)) if len(a.shape) == 2 else \
                    a[:, :, :, None].to_broadcast((*a.shape, n))

            def along(n, m=WINDOWS):
                return rows[:, n, :][:, None, :].to_broadcast((P, m, DIM))

            wide = acc[:, 0:WINDOWS, 0:DIM]
            stds = [0]

            def center(v):
                stds[0] += 1
                link(dve.tensor_reduce(st[:, 0, :], v, AX.X, ALU.add))
                link(dve.tensor_scalar(st[:, 0, :], st[:, 0, :], 1.0 / DIM, None, ALU.mult))
                link(dve.tensor_tensor(tmp[:, :, :], v, bc(st[:, 0, :], DIM), ALU.subtract))
                link(dve.tensor_tensor(wide, tmp[:, :, :], tmp[:, :, :], ALU.mult))
                dve.tensor_reduce(st[:, 1, :], wide, AX.X, ALU.add).then_inc(s_var, 1)
                dve.wait_ge(s_std, stds[0])
                link(dve.reciprocal(st[:, 2, :], st[:, 2, :]))

            def norm_relu():
                center(X[:, :, :])
                dve.scalar_tensor_tensor(out=Hn[:, :, :], in0=tmp[:, :, :], scalar=0.0, in1=bc(st[:, 2, :], DIM),
                                         op0=ALU.max, op1=ALU.mult).then_inc(s_h, 1)

            def copy_y(n):
                width = WIDE if n == 0 else DIM
                for c in range(CHUNKS):
                    v = n * CHUNKS + c
                    if n >= 3:
                        for j in range(CHUNK):
                            w = c * CHUNK + j
                            if w % 2 == 1:
                                u = (n - 3) * WINDOWS + w
                                dve.wait_ge(s_rooted, u + 1)
                                if u >= BANKS:
                                    dve.wait_ge(s_stage[u % BANKS], 16 * (u // BANKS))
                                dve.tensor_copy(stage[:, u % BANKS, :], ps[4 + w % 2][:, :]).then_inc(s_stc[1], 1)
                    dve.wait_ge(s_y, v + 1)
                    dve.tensor_copy(Y[:, c * CHUNK:(c + 1) * CHUNK, 0:width],
                                    ps[6 + v % 2][:, 0:CHUNK * WIDE].rearrange("p (w c) -> p w c", c=WIDE)[:, :, 0:width]
                                    ).then_inc(s_yc, 1)

            def split(v):
                link(dve.tensor_copy(tab[:, :, 0, :], v))
                link(dve.tensor_tensor(tres[:, :, :], v, tab[:, :, 0, :], ALU.subtract))
                link(dve.tensor_copy(tab[:, :, 1, :], tres[:, :, :]))
                link(dve.tensor_tensor(tab[:, :, 2, :], tres[:, :, :], tab[:, :, 1, :], ALU.subtract))

            def windows_for(eff):
                return eff

            link(dve.memset(X[:, WINDOWS - 1, :], 0.0))
            dve.memset(srcF[:, COLS:], 0.0)
            dve.memset(relsrcF[:, COLS:], 0.0)
            dve.memset(rel0[:, COLS:], -1.0)
            dve.memset(wint[0:1, 0, GROUPS:], 0)
            dve.memset(acc[:, WINDOWS:, :], 0.0)
            dve.memset(attn[:, WINDOWS:, :], 0.0)
            link(dve.memset(amax[:, WINDOWS:, :], 0.0))
            dve.sem_inc(s_xtail, 1)
            dve.wait_ge(s_const, 6)
            dve.wait_ge(s_edges, 64)
            dve.tensor_copy(iota[:, :], iota_i[:, :])
            dve.tensor_copy(iotab[:, :], iota_i[:, :])
            dve.tensor_copy(srcF[:, 0:COLS], srcI)
            dve.tensor_copy(typF[:, :], typI)
            link(dve.tensor_copy(dstF, dstI))
            dve.scalar_tensor_tensor(out=relsrcF[:, 0:COLS], in0=srcF[:, 0:COLS], scalar=float(RELS),
                                     in1=typF[:, :], op0=ALU.mult, op1=ALU.add)
            first = dstI[0:1, 0:COLS].rearrange("p (g k) -> p g k", k=K)[:, :, 0]
            link(dve.tensor_scalar(wint[0:1, 0, 0:GROUPS], first, 7, None, ALU.arith_shift_right))
            link(dve.tensor_copy(wrow[0:1, 0, :], wint[0:1, 0, 0:GROUPS]))
            link(dve.tensor_scalar(wrow[0:1, 1, :], wrow[0:1, 0, :], float(WINDOWS - SPAN), 0.0, ALU.min, ALU.max))
            link(dve.tensor_scalar(wrow[0:1, 2, :], wrow[0:1, 1, :], float(P), None, ALU.mult))
            dve.sem_inc(s_row, 1)

            def relative():
                link(dve.tensor_tensor(rel0[:, 0:COLS].rearrange("p (g k) -> p g k", k=K),
                                       dstF.rearrange("p (g k) -> p g k", k=K),
                                       bc(ps[7][:, 0:GROUPS], K), ALU.subtract))

            dve.wait_ge(s_rowb, 1)
            relative()
            link(dve.tensor_scalar(rel[:, 0:COLS], rel0[:, 0:COLS], -(SPAN * P - 1) / 2.0, None, ALU.add))
            link(dve.tensor_tensor(rel[:, 0:COLS], rel[:, 0:COLS], rel[:, 0:COLS], ALU.mult))
            link(dve.tensor_reduce(stat[:, 0:1], rel[:, 0:COLS - 1], AX.X, ALU.max))
            link(dve.tensor_tensor(stat[0:LAST, 0:1], stat[0:LAST, 0:1], rel[0:LAST, COLS - 1:COLS], ALU.max))

            dve.wait_ge(s_wts, 16 * 18)
            for n in range(2):
                for b in range(BASES):
                    bs = basis[:, n, b, :][:, None, :].to_broadcast((DIM, RELS, DIM))
                    cb = comp[:, n, :, b][:, :, None].to_broadcast((DIM, RELS, DIM))
                    d = Wr[:, n, 0:RELS, :]
                    t = tmp[0:DIM, 0:RELS, :]
                    if b == 0:
                        link(dve.tensor_tensor(d, bs, cb, ALU.mult))
                    else:
                        link(dve.tensor_tensor(t, bs, cb, ALU.mult))
                        link(dve.tensor_tensor(d, d, t, ALU.add))
            for n in range(2):
                link(dve.tensor_tensor(attw[:, n, :], att[:, n, :], W0[:, 0:DIM], ALU.mult))
                link(dve.tensor_reduce(W0[:, DIM + n * HEADS:DIM + (n + 1) * HEADS],
                                       attw[:, n, :].rearrange("p (h c) -> p h c", h=HEADS), AX.X, ALU.add))

            dve.wait_ge(s_x, 32)
            norm_relu()
            copy_y(0)
            dve.wait_ge(s_yc, CHUNKS)
            a_src, a_dst = Y[:, :, DIM:DIM + HEADS], Y[:, :, DIM + HEADS:WIDE]
            link(dve.tensor_reduce(stat[:, 1:5], a_src.rearrange("p w h -> p h w"), AX.X, ALU.max))
            link(dve.tensor_reduce(stat[:, 5:9], a_src.rearrange("p w h -> p h w"), AX.X, ALU.min))
            link(dve.tensor_scalar(stat[:, 5:9], stat[:, 5:9], -1.0, None, ALU.mult))
            dve.sem_inc(s_stat, 1)
            dve.wait_ge(s_statT, 1)
            link(dve.tensor_reduce(stv[:, :], ps[4][0:9, 0:P], AX.X, ALU.max))
            link(dve.tensor_scalar(stD[:, :], ident[0:9, 0:9], stv[:, 0:1], None, ALU.mult))
            dve.sem_inc(s_statD, 1)
            dve.wait_ge(s_statA, 1)
            link(dve.tensor_copy(stA[:, :], ps[5][:, 0:9]))
            link(dve.tensor_tensor(flag[:, 0:4], stA[:, 1:5], stA[:, 5:9], ALU.add))
            link(dve.tensor_reduce(flag[:, 4:5], flag[:, 0:4], AX.X, ALU.max))
            link(dve.tensor_scalar(flag[:, 5:6], flag[:, 4:5], RANGE, None, ALU.is_gt))
            link(dve.tensor_scalar(flag[:, 6:7], stA[:, 0:1], ((SPAN * P - 1) / 2.0) ** 2 + 1.0, None, ALU.is_gt))
            link(dve.tensor_tensor(flag[:, 7:8], flag[:, 5:6], flag[:, 6:7], ALU.max))
            link(dve.tensor_scalar(runs_i[0:1, :], flag[0:1, 7:8], float(RUNS - 1), 1.0, ALU.mult, ALU.add))
            link(dve.tensor_scalar(flag[0:1, 0:1], flag[0:1, 7:8], -1.0, 1.0, ALU.mult, ALU.add))
            link(dve.tensor_scalar(wrow[0:1, 1, :], wrow[0:1, 1, :], flag[0:1, 0:1], None, ALU.mult))
            link(dve.tensor_copy(wint[0:1, 0, 0:GROUPS], wrow[0:1, 1, :]))
            link(dve.tensor_scalar(wrow[0:1, 2, :], wrow[0:1, 1, :], float(P), None, ALU.mult))
            dve.sem_inc(s_row, 1)
            dve.wait_ge(s_rowb, 2)
            relative()
            link(dve.tensor_copy(amax[:, 0:WINDOWS, :], stA[:, 1:5][:, None, :].to_broadcast((P, WINDOWS, HEADS))))
            dve.sem_inc(s_runs, 1)
            runs = dve.value_load(runs_i[0:1, 0:1], min_val=1, max_val=RUNS)

            def start_windows():
                dve.tensor_copy(rel[:, :], rel0[:, :])
                link(dve.tensor_copy(wint[0:1, 1, :], wint[0:1, 0, :]))

            start_windows()
            with dve.If(runs > 1):
                mine = [0]

                def mlink(ins, at):
                    mine[0] += 1
                    ins.then_inc(m_step, 1)
                    dve.wait_ge(m_step, at + mine[0])

                Sf, Sn = before_rings[:, 0:256], before_rings[:, 256:512]
                Dg = before_rings[:, 512:1024].rearrange("p (h e) -> p h e", h=HEADS)
                Ii = before_rings[:, 1024:1536].rearrange("p (h e) -> p h e", h=HEADS)
                four = ident[:, None, :].to_broadcast((P, HEADS, P))
                mlink(dve.tensor_copy(Ii, four), 0)
                mlink(dve.tensor_copy(amax[:, 0:WINDOWS, :], a_src), 0)
                before = mine[0]
                STEPS = K * (2 + 2 * SPAN)
                with dve.Fori(0, RUNS) as r:
                    with dve.Fori(0, GROUPS) as g:
                        n = r * GROUPS + g
                        dve.wait_ge(m_gathered, (n + 1) * (K * 16))
                        w = dve.value_load(wint[0:1, 1, bass.ds(g, 1)], min_val=0, max_val=WPAD - SPAN)
                        mine[0] = before
                        at = n * STEPS + r * 2
                        for k in range(K):
                            mlink(dve.tensor_scalar(Sf, iota[:, :], rel[:, bass.ds(g * K + k, 1)], None,
                                                    ALU.is_equal), at)
                            dve.tensor_tensor(Dg, four, bc(G[:, 0, k, DIM:DIM + HEADS], P), ALU.mult)
                            mlink(dve.tensor_scalar(Sn, Sf, -1.0, BIG, ALU.add, ALU.mult), at)
                            dve.sem_inc(m_ready, 1)
                            dve.wait_ge(m_scored, n * K + k + 1)
                            for q in range(SPAN):
                                mlink(dve.tensor_reduce(sc[:, 0, 0:HEADS],
                                                        ps[q][:, :].rearrange("p (h e) -> p h e", h=HEADS),
                                                        AX.X, ALU.max), at)
                                to = amax[:, bass.ds(w + q, 1), :].rearrange("p a h -> p (a h)")
                                mlink(dve.tensor_tensor(to, to, sc[:, 0, 0:HEADS], ALU.max), at)
                            dve.sem_inc(m_taken, 1)
                    mine[0] = before
                    at = (r + 1) * (GROUPS * STEPS) + r * 2
                    mlink(dve.tensor_scalar(rel[:, :], rel[:, :], -float(SPAN * P), None, ALU.add), at)
                    mlink(dve.tensor_scalar(wint[0:1, 1, :], wint[0:1, 1, :], SPAN, None, ALU.add), at)
                    dve.sem_inc(s_maxed, 1)

            link(dve.tensor_copy(attn[:, 0:WINDOWS, 0:HEADS], a_dst))
            link(dve.tensor_tensor(ns[:, 0, 0:WINDOWS, :], amax[:, 0:WINDOWS, :], a_dst, ALU.add))
            link(dve.scalar_tensor_tensor(out=attn[:, 0:WINDOWS, HEADS:8], in0=ns[:, 0, 0:WINDOWS, :], scalar=SLOPE,
                                          in1=ns[:, 0, 0:WINDOWS, :], op0=ALU.mult, op1=ALU.max))
            split(attn[:, :, :])

            def edge_pass(p):
                link(dve.memset(acc[:, :, :], 0.0))
                start_windows()
                dve.sem_inc(p.begun, 1)
                with dve.Fori(0, RUNS) as r:
                    with dve.If(r < runs):
                        steps, base = [0], [0]

                        def plink(ins):
                            steps[0] += 1
                            ins.then_inc(p.step, 1)
                            dve.wait_ge(p.step, base[0] + steps[0])

                        def window(at):
                            return dve.value_load(wint[0:1, 1, bass.ds(at, 1)], min_val=0, max_val=WPAD - SPAN)

                        def one_hot(at, s, w):
                            if p.fetches:
                                dve.tensor_copy(tabw[:, s % 2, :, :],
                                                tab[:, bass.ds(w, SPAN), :, :].rearrange("p w a c -> p w (a c)"))
                            plink(dve.tensor_copy(relw[:, s % SLOTS, :], rel[:, bass.ds(at * K, K)]))
                            for k in range(K):
                                last = dve.tensor_scalar(S[:, s % SLOTS, k, :], iotab[:, :], relw[:, s % SLOTS, k:k + 1], None,
                                                         ALU.is_equal)
                            last.then_inc(p.onehot, 1)

                        def weigh(i, s):
                            num = r * GROUPS + i * SLOTS + s
                            cols = bass.ds((i * SLOTS + s) * K, K)
                            if p.kind == "count":
                                dve.tensor_tensor(Gb[:, s, :, PARTS * DIM:PARTS * DIM + RELS],
                                                  iota[:, 0:RELS][:, None, :].to_broadcast((P, K, RELS)),
                                                  bc(typF[:, cols], RELS), ALU.is_equal).then_inc(p.weighted, 1)
                                return
                            if p.fetches:
                                dve.wait_ge(p.fetched, r * (GROUPS + 1) + i * SLOTS + s + 1 + 2)
                                three = fetch_ps[s % 2][:, 0:24 * K].rearrange("p (k a c) -> p k a c", k=K, a=3)
                                plink(dve.tensor_copy(f1[:, :, :], three[:, :, 2, :]))
                                plink(dve.tensor_tensor(f2[:, :, :], f1[:, :, :], three[:, :, 1, :], ALU.add))
                                plink(dve.tensor_tensor(f1[:, :, :], f2[:, :, :], three[:, :, 0, :], ALU.add))
                            if p.kind == "relation":
                                plink(dve.tensor_tensor(sc[:, :, :],
                                                        iota[:, 0:RELS][:, None, :].to_broadcast((P, K, RELS)),
                                                        bc(typF[:, cols], RELS), ALU.is_equal))
                                plink(dve.tensor_tensor(sc[:, :, :], sc[:, :, :], f1[:, :, :], ALU.mult))
                                plink(dve.tensor_reduce(wt[:, :], sc[:, :, :], AX.X, ALU.add))
                            dve.wait_ge(p.gathered[s], (r * ITERS + i + 1) * (K * 16))
                            v = p.width
                            if p.kind == "attention":
                                plink(dve.tensor_tensor(sc[:, :, 0:HEADS], G[:, s, :, DIM:DIM + HEADS],
                                                        f1[:, :, 0:HEADS], ALU.add))
                                plink(dve.scalar_tensor_tensor(out=sc[:, :, HEADS:8], in0=sc[:, :, 0:HEADS],
                                                               scalar=SLOPE, in1=sc[:, :, 0:HEADS],
                                                               op0=ALU.mult, op1=ALU.max))
                                dve.tensor_tensor(sc[:, :, 0:HEADS], sc[:, :, HEADS:8],
                                                  f1[:, :, HEADS:8], ALU.subtract).then_inc(p.exp_in, 1)
                                dve.wait_ge(p.exp_out, num + 1)
                                dve.tensor_tensor(
                                    Wf[:, :, 0:DIM].rearrange("p k (h c) -> p k h c", h=HEADS),
                                    G[:, s, :, 0:DIM].rearrange("p k (h c) -> p k h c", h=HEADS),
                                    bc(Wf[:, :, DIM:DIM + HEADS], CH), ALU.mult).then_inc(p.whole, 1)
                            else:
                                weight = wt[:, :] if p.kind == "relation" else ew[:, cols]
                                dve.tensor_tensor(Wf[:, :, 0:DIM], G[:, s, :, 0:DIM],
                                                  bc(weight, DIM), ALU.mult).then_inc(p.whole, 1)
                            dve.wait_ge(p.high, num + 1)
                            dve.tensor_tensor(Rf[:, :, 0:v], Wf[:, :, 0:v], W3[:, s % 2, :, 0:v],
                                              ALU.subtract).then_inc(p.rest, 1)
                            dve.wait_ge(p.middle, num + 1)
                            dve.tensor_tensor(W3[:, s % 2, :, 2 * v:3 * v], Rf[:, :, 0:v], W3[:, s % 2, :, v:2 * v],
                                              ALU.subtract).then_inc(p.weighted, 1)

                        def add(i, s, w):
                            dve.wait_ge(p.summed, r * GROUPS + i * SLOTS + s + 1 + SLOTS)
                            v = p.width
                            got = summed_ps[s % 2][:, 0:SPAN * 204].rearrange("p (q c) -> p q c", q=SPAN)
                            sub = part[:, :, 0:v]
                            if p.kind == "count":
                                to = acc[:, bass.ds(w, SPAN), DIM:WIDE]
                                dve.tensor_tensor(to, to, got[:, :, PARTS * DIM:PARTS * DIM + RELS], ALU.add)
                            plink(dve.tensor_copy(sub, got[:, :, 2 * v:3 * v]))
                            plink(dve.tensor_tensor(sub, sub, got[:, :, v:2 * v], ALU.add))
                            plink(dve.tensor_tensor(sub, sub, got[:, :, 0:v], ALU.add))
                            to = acc[:, bass.ds(w, SPAN), 0:v]
                            plink(dve.tensor_tensor(to, to, sub, ALU.add))

                        PER_ITER = SLOTS * (5 + {"attention": 5, "relation": 6, "count": 0, "weight": 0}[p.kind])
                        PER_RUN = ITERS * PER_ITER + 3
                        base[0] = r * PER_RUN
                        one_hot(0, 0, window(0))
                        with dve.Fori(0, ITERS) as i:
                            base[0], steps[0] = r * PER_RUN + i * PER_ITER, 1
                            ws = [window(i * SLOTS + s) for s in range(SLOTS + 1)]
                            for s in range(SLOTS):
                                one_hot(i * SLOTS + s + 1, s + 1, ws[s + 1])
                                weigh(i, s)
                                if s > 0:
                                    add(i, s - 1, ws[s - 1])
                            add(i, SLOTS - 1, ws[SLOTS - 1])
                            assert steps[0] == 1 + PER_ITER
                        dve.tensor_scalar(rel[:, :], rel[:, :], -float(SPAN * P), None, ALU.add).then_inc(p.step, 1)
                        dve.tensor_scalar(wint[0:1, 1, :], wint[0:1, 1, :], SPAN, None, ALU.add).then_inc(p.step, 1)
                        dve.wait_ge(p.step, (r + 1) * PER_RUN)
                        dve.sem_inc(p.begun, 1)

            edge_pass(passes[0])
            link(dve.tensor_tensor(ns[:, 0, 0:WINDOWS, :], a_src, a_dst, ALU.add))
            link(dve.scalar_tensor_tensor(out=ns[:, 1, 0:WINDOWS, :], in0=ns[:, 0, 0:WINDOWS, :], scalar=SLOPE,
                                          in1=ns[:, 0, 0:WINDOWS, :], op0=ALU.mult, op1=ALU.max))
            link(dve.tensor_tensor(ns[:, 0, 0:WINDOWS, :], ns[:, 1, 0:WINDOWS, :], attn[:, 0:WINDOWS, HEADS:8],
                                   ALU.subtract))
            dve.sem_inc(s_self, 1)
            dve.wait_ge(s_pself, 1)
            pself = ns[:, 1, 0:WINDOWS, :]
            t4d = tmp[:, :, :].rearrange("p w (h c) -> p w h c", h=HEADS)
            dve.tensor_tensor(t4d, Y[:, :, 0:DIM].rearrange("p w (h c) -> p w h c", h=HEADS), bc(pself, CH), ALU.mult)
            link(dve.tensor_tensor(acc[:, 0:WINDOWS, DIM:DIM + HEADS], acc[:, 0:WINDOWS, DIM:DIM + HEADS], pself, ALU.add))
            link(dve.tensor_tensor(wide, wide, tmp[:, :, :], ALU.add))
            link(dve.reciprocal(ns[:, 0, 0:WINDOWS, :], acc[:, 0:WINDOWS, DIM:DIM + HEADS]))
            w4d = wide.rearrange("p w (h c) -> p w h c", h=HEADS)
            link(dve.tensor_tensor(t4d, w4d, bc(ns[:, 0, 0:WINDOWS, :], CH), ALU.mult))
            link(dve.tensor_tensor(tmp[:, :, :], tmp[:, :, :], along(0), ALU.add))
            link(dve.tensor_tensor(Hn[:, :, :], Hn[:, :, :], tmp[:, :, :], ALU.add))
            center(Hn[:, :, :])
            link(dve.tensor_tensor(tmp[:, :, :], tmp[:, :, :], bc(st[:, 2, :], DIM), ALU.mult))
            link(dve.tensor_tensor(tmp[:, :, :], tmp[:, :, :], along(1), ALU.mult))
            link(dve.tensor_tensor(tmp[:, :, :], tmp[:, :, :], along(2), ALU.add))
            link(dve.tensor_tensor(X[:, :, :], X[:, :, :], tmp[:, :, :], ALU.add))

            norm_relu()
            copy_y(1)
            dve.wait_ge(s_yc, 2 * CHUNKS)
            for c in range(CHUNKS):
                ws = slice(c * CHUNK, (c + 1) * CHUNK)
                link(dve.tensor_copy(rows3[:, ws, 0, :], Y[:, ws, 0:DIM]))
                link(dve.tensor_tensor(tmp[:, ws, :], Y[:, ws, 0:DIM], rows3[:, ws, 0, :], ALU.subtract))
                link(dve.tensor_copy(rows3[:, ws, 1, :], tmp[:, ws, :]))
                dve.tensor_tensor(rows3[:, ws, 2, :], tmp[:, ws, :], rows3[:, ws, 1, :],
                                  ALU.subtract).then_inc(s_rows3, 1)
            dve.wait_ge(s_table[1], 16 * CHUNKS)
            edge_pass(passes[1])
            counts = acc[:, :, DIM:WIDE]
            link(dve.tensor_reduce(st[:, 2, :], acc[:, 0:WINDOWS, DIM:WIDE], AX.X, ALU.add))
            link(dve.tensor_scalar(st[:, 0, :], st[:, 2, :], 1.0, 1.0, ALU.add, ALU.max))
            dve.sem_inc(s_self, 1)
            link(dve.tensor_scalar(inv[:, :, :], counts, 1.0, None, ALU.max))
            link(dve.reciprocal(inv[:, :, :], inv[:, :, :]))
            split(inv[:, :, :])
            dve.wait_ge(s_pself, 2)
            link(dve.reciprocal(st[:, 0, :], st[:, 1, :]))
            link(dve.tensor_tensor(tmp[:, :, :], wide, Y[:, :, 0:DIM], ALU.add))
            link(dve.tensor_tensor(tmp[:, :, :], tmp[:, :, :], bc(st[:, 0, :], DIM), ALU.mult))
            link(dve.tensor_tensor(tmp[:, :, :], tmp[:, :, :], along(3), ALU.add))
            link(dve.tensor_tensor(X[:, :, :], X[:, :, :], tmp[:, :, :], ALU.add))

            norm_relu()
            copy_y(2)
            dve.wait_ge(s_yc, 3 * CHUNKS)
            edge_pass(passes[2])
            link(dve.tensor_tensor(tmp[:, :, :], wide, along(4), ALU.add))
            link(dve.tensor_tensor(X[:, :, :], X[:, :, :], tmp[:, :, :], ALU.add))

            norm_relu()
            copy_y(3)
            dve.wait_ge(s_yc, 4 * CHUNKS)
            for b in range(BANKS):
                dve.wait_ge(s_stage[b], 16 * len(range(b, WINDOWS, BANKS)))
            edge_pass(passes[3])
            link(dve.tensor_tensor(tmp[:, :, :], wide, Y[:, :, 0:DIM], ALU.add))
            link(dve.tensor_tensor(tmp[:, :, :], tmp[:, :, :], along(5), ALU.add))
            dve.tensor_scalar(Hn[:, :, :], tmp[:, :, :], 0.0, None, ALU.max).then_inc(s_h, 1)
            copy_y(4)
            dve.wait_ge(s_yc, 5 * CHUNKS)
            for b in range(BANKS):
                dve.wait_ge(s_stage[b], 16 * len(range(b, 2 * WINDOWS, BANKS)))
            edge_pass(passes[4])
            link(dve.tensor_tensor(tmp[:, :, :], wide, Y[:, :, 0:DIM], ALU.add))
            link(dve.tensor_tensor(tmp[:, :, :], tmp[:, :, :], along(6), ALU.add))
            link(dve.tensor_tensor(X[:, :, :], X[:, :, :], tmp[:, :, :], ALU.add))
            dve.sem_inc(s_out, 1)


_INS = ['x', 'src', 'dst', 'edge_type_8', 'edge_weight', 'L0_gnn_W', 'L0_gnn_att_src', 'L0_gnn_att_dst',
        'L0_gnn_bias', 'L0_gnn_gamma', 'L0_gnn_beta', 'L1_gnn_weight', 'L1_gnn_bias', 'L2_gnn_W', 'L2_gnn_b',
        'L3_gnn_basis1', 'L3_gnn_comp1', 'L3_gnn_root1', 'L3_gnn_bias1', 'L3_gnn_basis2', 'L3_gnn_comp2',
        'L3_gnn_root2', 'L3_gnn_bias2']


def kernel(**inputs):
    import numpy as _np
    import concourse.bacc as _bacc
    from concourse import mybir as _mybir
    from concourse.bass_utils import run_bass_kernel_spmd as _run

    def by_column(a, fill):
        full = _np.full(COLS * P, fill, a.dtype)
        full[:EDGES] = a
        return full.reshape(COLS, P).T

    nc = _bacc.Bacc("TRN2", target_bir_lowering=False, num_devices=1)
    arrays, args = {}, []
    for name in _INS:
        a = _np.asarray(inputs[name])
        if name in ("src", "edge_type_8", "edge_weight"):
            a = by_column(a, 0)
        if name == "dst":
            a = by_column(a, PADNODE)
        if name in ("L1_gnn_weight", "L2_gnn_W"):
            a = a.T
        a = _np.ascontiguousarray(a)
        arrays[f"in_{name}"] = a
        args.append(nc.dram_tensor(f"in_{name}", a.shape, _mybir.dt.from_np(a.dtype), kind="ExternalInput").ap())
    args.append(nc.dram_tensor("out_x", (NODES, DIM), _mybir.dt.float32, kind="ExternalOutput").ap())
    gnn_stack(nc, *args)
    r = _run(nc, [arrays], core_ids=[0])
    return r.results[0]["out_x"]
```

```python
import concourse.bass as bass
from concourse import mybir
from contextlib import ExitStack

NODES = 6250
EDGES = 206250
DIM = 64
HEADS = 4
CH = DIM // HEADS
RELS = 8
BASES = 4
SLOPE = 0.2
EPS = 1e-5

P = 128
WINDOWS = -(-NODES // P)
TAIL = NODES - (WINDOWS - 1) * P
ROWS = WINDOWS * P
COLS = -(-EDGES // P)
LAST = EDGES - (COLS - 1) * P
K = 13
GROUPS = COLS // K
SLOTS = 4
ITERS = GROUPS // SLOTS
AHEAD = SLOTS * K
SPAN = 2
RUNS = -(-WINDOWS // SPAN)
WPAD = RUNS * SPAN
assert GROUPS * K == COLS and ITERS * SLOTS == GROUPS
PADNODE = ROWS - 1
assert PADNODE >= NODES
WIDE = DIM + 8
CHUNK = 7
CHUNKS = WINDOWS // CHUNK
assert CHUNK * CHUNKS == WINDOWS
HALVES = (slice(0, 4 * CHUNK), slice(4 * CHUNK, WINDOWS))
BANKS = 4
FLIPS = -(-K // 4)
PARTS = 3
assert FLIPS == BANKS
BIG = 1e30
RANGE = 80.0
PRIME = 8191
HASHES = 3
HASH_SCALES = (1021.0, 1493.0, 1879.0)
HASH_OFFSETS = (2711.0, 1283.0, 3557.0)
ROUND = 1.5 * 2.0 ** 23
assert ROWS * 2000 < 2 ** 24 and GROUPS * RUNS * 2 * PRIME // SLOTS < 2 ** 24


def gnn_stack(nc, x, src, dst, etype, eweight, w0, att_src, att_dst, bias0, gamma0, beta0, w1t, b1, w2t, b2,
              basis1, comp1, root1, bias1, basis2, comp2, root2, bias2, out):
    f32, i32, bf16 = mybir.dt.float32, mybir.dt.int32, mybir.dt.bfloat16
    ALU, ACT, AX = mybir.AluOpType, mybir.ActivationFunctionType, mybir.AxisListType

    t0 = nc.dram_tensor("rows_l0", (ROWS, DIM + HEADS), f32, kind="Internal").ap()
    t1 = nc.dram_tensor("rows_l1", (ROWS, DIM), f32, kind="Internal").ap()
    t2 = nc.dram_tensor("rows_l2", (ROWS, DIM), f32, kind="Internal").ap()
    t3 = nc.dram_tensor("rows_l3a", (ROWS * RELS, DIM), f32, kind="Internal").ap()
    t4 = nc.dram_tensor("rows_l3b", (ROWS * RELS, DIM), f32, kind="Internal").ap()

    ctx = ExitStack()
    with ctx:
        def sb(name, shape, dt=f32):
            return ctx.enter_context(nc.sbuf_tensor(name, shape, dt))

        def sem(name):
            return ctx.enter_context(nc.semaphore(name))

        X = sb("X", [P, WINDOWS, DIM])
        Hn = sb("Hn", [P, WINDOWS, DIM])
        Y = sb("Y", [P, WINDOWS, WIDE])
        acc = sb("acc", [P, WPAD, WIDE])
        tmp = sb("tmp", [P, WINDOWS, DIM])
        st = sb("st", [P, 3, WINDOWS])
        attn = sb("attn", [P, WPAD, 8])
        ns = sb("ns", [P, 2, WPAD, HEADS])
        amax = sb("amax", [P, WPAD, HEADS])
        tab = sb("tab", [P, WPAD, 3, 8], bf16)
        tres = sb("tres", [P, WPAD, 8])
        srcF = sb("srcF", [P, COLS + AHEAD])
        relsrcF = sb("relsrcF", [P, COLS + AHEAD])
        typF = sb("typF", [P, COLS])
        ew = sb("ew", [P, COLS])
        rel0 = sb("rel0", [P, COLS + K])
        rel = sb("rel", [P, COLS + K])
        idx = sb("idx", [P, SLOTS, K], i32)
        WG = DIM + HEADS
        Gall = sb("G", [P, max(SLOTS * K * WG, WINDOWS * PARTS * DIM // 2)])
        G = Gall[:, 0:SLOTS * K * WG].rearrange("p (s k c) -> p s k c", s=SLOTS, k=K)
        onehots = sb("onehots", [P, (SLOTS + 2) * K * SPAN * P], bf16)
        S = onehots[:, 0:SLOTS * K * SPAN * P].rearrange("p (a k j) -> p a k j", a=SLOTS, k=K)
        ST = onehots[:, SLOTS * K * SPAN * P:].rearrange("p (a k j) -> p a k j", a=2, k=K)
        before_rings = onehots[:, :].bitcast(f32)
        Wf = sb("Wf", [P, K, DIM + HEADS])
        Rf = sb("Rf", [P, K, DIM + HEADS])
        W3 = sb("W3", [P, 2, K, PARTS * (DIM + HEADS)], bf16)
        relw = sb("relw", [P, SLOTS, K])
        part = sb("part", [P, SPAN, DIM + HEADS])
        tabw = sb("tabw", [P, 2, SPAN, 24], bf16)
        in_Wf = Wf[:, :, :].rearrange("p k c -> p (k c)")
        HEDGES = AHEAD // 2
        HCOLS = 2 * HEDGES
        assert AHEAD * ITERS == COLS
        hsum, ends, hx, hx2, hq = (in_Wf[:, a * HEDGES:b * HEDGES] for a, b in (
            (0, HASHES), (HASHES, HASHES + 2), (HASHES + 2, 3 * HASHES + 2), (3 * HASHES + 2, 5 * HASHES + 2),
            (5 * HASHES + 2, 7 * HASHES + 2)))
        f1 = sb("f1", [P, K, 8])
        sc = sb("sc", [P, K, 8])
        wt = sb("wt", [P, K])
        ident = sb("ident", [P, P])
        identb = sb("identb", [P, P], bf16)
        ones = sb("ones", [P, P])
        iota_i = sb("iota_i", [P, SPAN * P], i32)
        iota = sb("iota", [P, SPAN * P])
        iotab = sb("iotab", [P, SPAN * P], bf16)
        epsc = sb("epsc", [P, 1])
        onec = sb("onec", [P, 1])
        rows = sb("rows", [P, 7, DIM])
        WCOLS = WIDE + 2 * DIM + 2 * (RELS + 1) * DIM
        Wparts = sb("Wparts", [P, PARTS, WCOLS], bf16)
        WSTART = [0, WIDE, WIDE + DIM, WIDE + 2 * DIM, WIDE + 2 * DIM + (RELS + 1) * DIM]
        at_first = acc[:, :, :].rearrange("p w c -> p (w c)")
        basis = at_first[:, 0:2 * BASES * DIM].rearrange("p (n b o) -> p n b o", n=2, b=BASES)
        comp = at_first[:, 512:512 + 2 * RELS * BASES].rearrange("p (n r b) -> p n r b", n=2, r=RELS)
        att = at_first[:, 640:640 + 2 * DIM].rearrange("p (n c) -> p n c", n=2)
        attw = at_first[:, 768:768 + 2 * DIM].rearrange("p (n c) -> p n c", n=2)
        Wall = at_first[:, 896:896 + WCOLS]
        Wrest = at_first[:, 896 + WCOLS:896 + WCOLS + (WCOLS - WSTART[3])]
        Wterm = Wrest[:, RELS * DIM:2 * RELS * DIM].rearrange("p (r o) -> p r o", r=RELS)
        W0 = Wall[:, 0:WIDE]
        Wr = Wall[:, WSTART[3]:].rearrange("p (n r o) -> p n r o", n=2, r=RELS + 1)
        wrow = sb("wrow", [1, 4, GROUPS])
        wint = sb("wint", [1, 2, GROUPS + 1], i32)
        stat = sb("stat", [P, 9])
        stT = sb("stT", [9, P])
        stv = sb("stv", [9, 1])
        stD = sb("stD", [9, 9])
        stA = sb("stA", [P, 9])
        flag = sb("flag", [P, 8])
        runs_i = sb("runs_i", [1, 1], i32)
        turned_i = sb("turned_i", [1, 1], i32)

        dstI, srcI, typI, dstF = (before_rings[:, n * COLS:(n + 1) * COLS] for n in range(4))
        dstI, srcI, typI = (v.bitcast(i32) for v in (dstI, srcI, typI))
        stage = before_rings[:, 0:BANKS * RELS * DIM].rearrange("p (b n) -> p b n", b=BANKS)
        hT = onehots[:, (SLOTS + 2) * K * SPAN * P - 2 * CHUNK * SPAN * P:]\
            .rearrange("p (a w b n) -> p a w b n", a=2, w=CHUNK, b=2)
        Hp = Gall[:, 0:WINDOWS * PARTS * DIM // 2].bitcast(bf16).rearrange("p (w c) -> p w c", w=WINDOWS)

        ps = [ctx.enter_context(nc.psum_tensor(f"ps{i}", [P, 512], f32)) for i in range(8)]
        flip = ps[0:4]
        flipb = [b[:, :].bitcast(bf16) for b in flip]
        summed_ps = ps[4:6]
        fetch_ps = ps[6:8]

        s_load = sem("s_load")
        s_edges = sem("s_edges")
        s_x = sem("s_x")
        s_xtail = sem("s_xtail")
        s_wts = sem("s_wts")
        s_wts3 = sem("s_wts3")
        s_wr = sem("s_wr")
        s_const = sem("s_const")
        s_pool = sem("s_pool")
        s_dve = sem("s_dve")
        s_var = sem("s_var")
        s_std = sem("s_std")
        s_centered = sem("s_centered")
        s_squared = sem("s_squared")
        s_h = sem("s_h")
        s_h1 = sem("s_h1")
        s_hrest = sem("s_hrest")
        s_h2 = sem("s_h2")
        s_hparts = sem("s_hparts")
        s_w = sem("s_w")
        s_hT = sem("s_hT")
        s_hTc = sem("s_hTc")
        s_y = sem("s_y")
        s_yc = sem("s_yc")
        s_row = sem("s_row")
        s_rowb = sem("s_rowb")
        s_stat = sem("s_stat")
        s_statT = sem("s_statT")
        s_statD = sem("s_statD")
        s_statA = sem("s_statA")
        s_runs = sem("s_runs")
        s_maxed = sem("s_maxed")
        s_gathering = sem("s_gathering")
        s_hashed = sem("s_hashed")
        s_hashsum = sem("s_hashsum")
        s_turned = sem("s_turned")
        s_stc = [sem("s_stc_act"), sem("s_stc_dve")]
        s_rooted = sem("s_rooted")
        s_rootc = sem("s_rootc")
        s_table = [sem(f"s_table{n}") for n in range(5)]
        s_stage = [sem(f"s_stage{n}") for n in range(BANKS)]
        s_self = sem("s_self")
        s_pself = sem("s_pself")
        s_out = sem("s_out")

        class Pass:
            def __init__(self, n, kind, table, width, summed_width, order):
                self.n, self.kind, self.table, self.width = n, kind, table, width
                self.summed_width, self.order = summed_width, order
                self.fetches = kind in ("attention", "relation")
                self.begun = sem(f"p{n}_begun")
                self.idx_ready = sem(f"p{n}_idx_ready")
                self.gathered = [sem(f"p{n}_gathered{s}") for s in range(SLOTS)]
                self.onehot = sem(f"p{n}_onehot")
                if self.fetches:
                    self.flipped = sem(f"p{n}_flipped")
                    self.flip_copied = sem(f"p{n}_flip_copied")
                    self.fetched = sem(f"p{n}_fetched")
                if kind == "attention":
                    self.exp_in = sem(f"p{n}_exp_in")
                    self.exp_out = sem(f"p{n}_exp_out")
                self.whole = sem(f"p{n}_whole")
                self.high = sem(f"p{n}_high")
                self.rest = sem(f"p{n}_rest")
                self.middle = sem(f"p{n}_middle")
                self.weighted = sem(f"p{n}_weighted")
                self.summed = sem(f"p{n}_summed")
                self.step = sem(f"p{n}_step")
                self.before = 0

        passes = [
            Pass(0, "attention", t0, DIM + HEADS, DIM + HEADS, srcF),
            Pass(1, "count", t1, DIM, WIDE, srcF),
            Pass(2, "weight", t2, DIM, DIM, srcF),
            Pass(3, "relation", t3, DIM, DIM, relsrcF),
            Pass(4, "relation", t4, DIM, DIM, relsrcF),
        ]
        backwards = Pass("1b", "count", t1, DIM, WIDE, relsrcF)
        backwards.before = 3
        m_idx = sem("m_idx")
        m_gathered = sem("m_gathered")
        m_ready = sem("m_ready")
        m_scored = sem("m_scored")
        m_taken = sem("m_taken")
        m_step = sem("m_step")

        block = ctx.enter_context(nc.Block())

        @block.sync
        def _(sp):
            sp.dma_start(X[:, 0:WINDOWS - 1, :],
                         x[0:(WINDOWS - 1) * P, :].rearrange("(w p) c -> p w c", p=P)).then_inc(s_x, 16)
            sp.wait_ge(s_xtail, 1)
            sp.dma_start(X[0:TAIL, WINDOWS - 1, :], x[(WINDOWS - 1) * P:NODES, :]).then_inc(s_x, 16)
            sp.dma_start(dstI, dst).then_inc(s_edges, 16)
            sp.dma_start(srcI, src).then_inc(s_edges, 16)
            sp.dma_start(typI, etype).then_inc(s_edges, 16)
            sp.dma_start(ew[:, :], eweight).then_inc(s_edges, 16)
            for n, v in enumerate((bias0, gamma0, beta0, b1, b2, bias1, bias2)):
                sp.dma_start(rows[:, n, :], v.rearrange("(a c) -> a c", a=1).to_broadcast((P, DIM))).then_inc(s_wts3, 16)
            for n, (b, c, rt) in enumerate(((basis1, comp1, root1), (basis2, comp2, root2))):
                for half in (slice(0, DIM), slice(DIM, P)):
                    sp.dma_start(basis[half, n, :, :], b.rearrange("b i o -> i b o")).then_inc(s_wts3, 16)
                    sp.dma_start(Wr[half, n, RELS, :], rt).then_inc(s_wts3, 16)
                sp.dma_start(comp[:, n, :, :].rearrange("p r b -> p (r b)"),
                             c.rearrange("r b -> (r b)").rearrange("(a c) -> a c", a=1)
                             .to_broadcast((P, RELS * BASES))).then_inc(s_wts3, 16)
            for n in range(3):
                tv = passes[n].table.rearrange("(w p) c -> p w c", p=P)
                for c in range(CHUNKS):
                    ws = slice(c * CHUNK, (c + 1) * CHUNK)
                    sp.wait_ge(s_yc, n * CHUNKS + c + 1)
                    sp.dma_start(tv[:, ws, :], Y[:, ws, 0:passes[n].width]).then_inc(s_table[n], 16)
            for n in (3, 4):
                tv = passes[n].table.rearrange("(w p r) c -> w p (r c)", p=P, r=RELS)
                for w in range(WINDOWS):
                    v = (n - 3) * WINDOWS + w
                    sp.wait_ge(s_stc[w % 2], (n - 3) * ((WINDOWS + 1 - w % 2) // 2) + w // 2 + 1)
                    sp.dma_start(tv[w, :, :], stage[:, v % BANKS, :]).then_inc(s_stage[v % BANKS], 16)
            sp.wait_ge(s_out, 1)
            sp.dma_start(out[0:(WINDOWS - 1) * P, :].rearrange("(w p) c -> p w c", p=P),
                         acc[:, 0:WINDOWS - 1, 0:DIM]).then_inc(s_load, 16)
            sp.dma_start(out[(WINDOWS - 1) * P:NODES, :], acc[0:TAIL, WINDOWS - 1, 0:DIM]).then_inc(s_load, 16)
            sp.wait_ge(s_load, 32)
            for n in range(3):
                sp.wait_ge(s_table[n], 16 * CHUNKS)
            for b in range(BANKS):
                sp.wait_ge(s_stage[b], 16 * len(range(b, 2 * WINDOWS, BANKS)))

        @block.gpsimd
        def _(pool):
            pool.iota(iota_i[:, :], [[1, SPAN * P]], base=0, channel_multiplier=0).then_inc(s_const, 1)
            pool.memset(ident[:, :], 0.0).then_inc(s_pool, 1)
            pool.memset(ones[:, :], 1.0).then_inc(s_const, 1)
            pool.memset(epsc[:, :], EPS).then_inc(s_const, 1)
            pool.memset(onec[:, :], 1.0).then_inc(s_const, 1)
            pool.memset(identb[:, :], 0.0).then_inc(s_pool, 1)
            pool.wait_ge(s_pool, 2)
            for m in (ident, identb):
                pool.affine_select(out=m[:, :], in_=m[:, :], compare_op=ALU.not_equal, fill=1.0,
                                   base=0, pattern=[[-1, P]], channel_multiplier=1).then_inc(s_const, 1)
            pool.wait_ge(s_wts3, 16 * 17)
            made = 0
            for n in range(2):
                for b in range(BASES):
                    of_base = basis[:, n, b, :][:, None, :].to_broadcast((P, RELS, DIM))
                    of_relation = comp[:, n, :, b][:, :, None].to_broadcast((P, RELS, DIM))
                    total = Wr[:, n, 0:RELS, :]
                    term = total if b == 0 else Wterm
                    pool.tensor_tensor(term, of_base, of_relation, ALU.mult).then_inc(s_wr, 1)
                    made += 1
                    pool.wait_ge(s_wr, made)
                    if b > 0:
                        pool.tensor_tensor(total, total, term, ALU.add).then_inc(s_wr, 1)
                        made += 1
                        pool.wait_ge(s_wr, made)
            pool.wait_ge(s_runs, 1)
            runs = pool.value_load(runs_i[0:1, 0:1], min_val=1, max_val=RUNS)

            pool.wait_ge(s_table[0], 16 * CHUNKS)
            with pool.If(runs > 1):
                with pool.Fori(0, RUNS) as r:
                    with pool.Fori(0, GROUPS) as g:
                        pool.wait_ge(m_idx, r * GROUPS + g + 1)
                        pool.sem_inc(s_gathering, 1)
                        for k in range(K):
                            pool.indirect_dma_start(
                                G[:, 0, k, 0:DIM + HEADS], None, t0,
                                bass.IndirectOffsetOnAxis(ap=idx[:, 0, k:k + 1], axis=0)).then_inc(m_gathered, 16)

            for p in passes:
                if p.n < 3:
                    pool.wait_ge(s_table[p.n], 16 * CHUNKS)
                else:
                    for b in range(BANKS):
                        pool.wait_ge(s_stage[b], 16 * len(range(b, (p.n - 2) * WINDOWS, BANKS)))
                def run(r, p=p):
                    with pool.Fori(0, ITERS) as i:
                        for s in range(SLOTS):
                            pool.wait_ge(p.idx_ready, r * (GROUPS + SLOTS) + i * SLOTS + s + 1)
                            pool.wait_ge(p.summed, r * GROUPS + i * SLOTS + s + 1)
                            pool.sem_inc(s_gathering, 1)
                            for k in range(K):
                                pool.indirect_dma_start(
                                    G[:, s, k, 0:p.width], None, p.table,
                                    bass.IndirectOffsetOnAxis(ap=idx[:, s, k:k + 1], axis=0)
                                ).then_inc(p.gathered[s], 16)

                run(0)
                with pool.If(runs > 1):
                    with pool.Fori(1, RUNS) as r:
                        run(r)
                if p.kind == "count":
                    pool.wait_ge(s_turned, 1)
                    turned = pool.value_load(turned_i[0:1, 0:1], min_val=0, max_val=1)
                    with pool.If(turned > 0):
                        with pool.Fori(0, RUNS) as r:
                            run(r, backwards)

        @block.scalar
        def _(act):
            for n, v in enumerate((att_src, att_dst)):
                act.dma_start(att[:, n, :], v.rearrange("h c -> (h c)").rearrange("(a c) -> a c", a=1)
                              .to_broadcast((P, DIM))).then_inc(s_wts, 16)
            for to, v in ((W0[:, 0:DIM], w0), (Wall[:, WSTART[1]:WSTART[2]], w1t), (Wall[:, WSTART[2]:WSTART[3]], w2t)):
                act.dma_start(to[0:DIM], v).then_inc(s_wts, 16)
                act.dma_start(to[DIM:P], v).then_inc(s_wts, 16)
            def squares_and_roots(n):
                for h, ws in enumerate(HALVES):
                    act.wait_ge(s_centered, 2 * n + h + 1)
                    act.activation(Y[:, ws, 0:DIM], tmp[:, ws, :], ACT.Square).then_inc(s_squared, 1)
                for h, ws in enumerate(HALVES):
                    act.wait_ge(s_var, 2 * n + h + 1)
                    act.activation(st[:, 2, ws], st[:, 1, ws], ACT.Sqrt, bias=epsc[:, 0:1],
                                   scale=1.0 / DIM).then_inc(s_std, 1)

            def parts_of_h(n):
                for h, ws in enumerate(HALVES):
                    act.wait_ge(s_h, 2 * n + h + 1)
                    act.activation(Hp[:, ws, DIM:2 * DIM], Hn[:, ws, :], ACT.Copy).then_inc(s_h1, 1)
                for h, ws in enumerate(HALVES):
                    act.wait_ge(s_hrest, 2 * n + h + 1)
                    act.activation(Hp[:, ws, 2 * DIM:3 * DIM], tmp[:, ws, :], ACT.Copy).then_inc(s_h2, 1)

            def copy_turned(n):
                def copy_part(c, b):
                    v = n * CHUNKS + c
                    a, z = ((0, 4), (4, CHUNK))[b]
                    act.wait_ge(s_hT, v + 1)
                    if v >= 2:
                        act.wait_ge(s_y, v - 1)
                    act.activation(hT[:, v % 2, a:z, :, :].rearrange("p w b n -> p (w b n)"),
                                   flipb[b + 2 * (v % 2)][:, 0:(z - a) * 2 * P], ACT.Copy).then_inc(s_hTc, 1)

                for b in range(2):
                    copy_part(0, b)
                for c in range(CHUNKS):
                    todo = [(c + 1, b) for b in range(2)] if c + 1 < CHUNKS else []
                    for w in range(c * CHUNK, (c + 1) * CHUNK):
                        if n >= 3 and w % 2 == 0:
                            stage_window(n, w)
                            if todo:
                                copy_part(*todo.pop(0))
                    for part_of_chunk in todo:
                        copy_part(*part_of_chunk)

            def stage_window(n, w):
                u = (n - 3) * WINDOWS + w
                act.wait_ge(s_rooted, u + 1)
                if u >= BANKS:
                    act.wait_ge(s_stage[u % BANKS], 16 * (u // BANKS))
                act.activation(stage[:, u % BANKS, :], ps[4 + w % 2][:, :], ACT.Copy).then_inc(s_stc[0], 1)

            act.wait_ge(s_const, 6)
            squares_and_roots(0)
            parts_of_h(0)
            copy_turned(0)
            act.wait_ge(s_runs, 1)
            runs = act.value_load(runs_i[0:1, 0:1], min_val=1, max_val=RUNS)
            with act.If(runs > 1):
                act.sem_inc(m_taken, K)
                with act.Fori(0, RUNS) as r:
                    with act.Fori(0, GROUPS) as g:
                        act.wait_ge(m_taken, (r * GROUPS + g + 1) * K)
                        act.activation(idx[:, 0, :], srcF[:, bass.ds(g * K, K)], ACT.Copy).then_inc(m_idx, 1)
                act.wait_ge(m_taken, (RUNS * GROUPS + 1) * K)

            for p in passes:
                act.wait_ge(p.begun, 1)
                if p.fetches:
                    act.sem_inc(p.flip_copied, BANKS)
                def run(r, p=p):
                    for s in range(SLOTS):
                        if s == 0:
                            act.wait_ge(p.begun, r + 1)
                        act.activation(idx[:, s, :], p.order[:, s * K:(s + 1) * K], ACT.Copy).then_inc(p.idx_ready, 1)
                    if p.kind == "attention" and isinstance(r, int):
                        act.wait_ge(s_self, 1)
                        act.activation(ns[:, 1, 0:WINDOWS, :], ns[:, 0, 0:WINDOWS, :], ACT.Exp).then_inc(s_pself, 1)

                    def copy_flips(chunks, at, s):
                        for c in chunks:
                            m = min(4, K - 4 * c)
                            act.wait_ge(p.flipped, at * FLIPS + c + 1)
                            act.activation(ST[:, s % 2, 4 * c:4 * c + m, :].rearrange("p k j -> p (k j)"),
                                           flipb[c][:, 0:m * SPAN * P], ACT.Copy).then_inc(p.flip_copied, 1)

                    if p.fetches:
                        act.wait_ge(p.fetched, r * (GROUPS + 1) + 1)
                        copy_flips(range(FLIPS), r * (GROUPS + 1), 0)
                    with act.Fori(0, ITERS) as i:
                        for s in range(SLOTS):
                            n = r * GROUPS + i * SLOTS + s
                            ahead = r * (GROUPS + 1) + i * SLOTS + s + 1
                            if p.fetches:
                                act.wait_ge(p.fetched, ahead + 1)
                                copy_flips((0,), ahead, s + 1)
                            act.wait_ge(p.gathered[s], (r * ITERS + i + 1) * (K * 16))
                            act.activation(idx[:, s, :], p.order[:, bass.ds((i * SLOTS + s + SLOTS) * K, K)],
                                           ACT.Copy).then_inc(p.idx_ready, 1)
                            if p.kind == "attention":
                                act.wait_ge(p.exp_in, n + 1)
                                act.activation(Wf[:, :, DIM:DIM + HEADS], sc[:, :, 0:HEADS],
                                               ACT.Exp).then_inc(p.exp_out, 1)
                            if p.fetches:
                                copy_flips((1,), ahead, s + 1)
                            v = p.width
                            act.wait_ge(p.whole, n + 1)
                            weighted = G[:, s, :, 0:v] if p.kind == "count" else Wf[:, :, 0:v]
                            act.activation(W3[:, s % 2, :, 0:v], weighted, ACT.Copy).then_inc(p.high, 1)
                            if p.fetches:
                                copy_flips((2,), ahead, s + 1)
                            act.wait_ge(p.rest, n + 1)
                            act.activation(W3[:, s % 2, :, v:2 * v], Rf[:, :, 0:v], ACT.Copy).then_inc(p.middle, 1)
                            if p.fetches:
                                copy_flips((3,), ahead, s + 1)
                run(0)
                with act.If(runs > 1):
                    with act.Fori(1, RUNS) as r:
                        run(r)
                if p.kind == "count":
                    act.wait_ge(s_turned, 1)
                    turned = act.value_load(turned_i[0:1, 0:1], min_val=0, max_val=1)
                    with act.If(turned > 0):
                        with act.Fori(0, RUNS) as r:
                            run(r, backwards)
                if p.kind == "attention":
                    squares_and_roots(1)
                if p.kind == "count":
                    act.wait_ge(s_self, 2)
                    act.activation(st[:, 1, :], st[:, 0, :], ACT.Sqrt).then_inc(s_pself, 1)
                if p.n < 3:
                    squares_and_roots(p.n + 2)
                if p.n < 4:
                    parts_of_h(p.n + 1)
                    copy_turned(p.n + 1)

        @block.tensor
        def _(pe):
            def turn(n):
                width = (WIDE, DIM, DIM, RELS * DIM, RELS * DIM)[n]

                def flips(c):
                    v = n * CHUNKS + c
                    pe.wait_ge(s_hparts, 2 * n + (1 if c < 4 else 2))
                    if v >= 2:
                        pe.wait_ge(s_hTc, 2 * (v - 1))
                    for j in range(CHUNK):
                        for b in range(2):
                            to = (2 * (j % 4) + b) * P
                            last = pe.transpose(flipb[j // 4 + 2 * (v % 2)][:, to:to + P],
                                                Hp[:, c * CHUNK + j, (1 - b) * DIM:(3 - b) * DIM], identb[:, :])
                    last.then_inc(s_hT, 1)

                def product(to, v, j, at, cols):
                    for part_of_w in range(PARTS):
                        last = pe.matmul(to, hT[:, v % 2, j, part_of_w // 2, :],
                                         Wparts[:, part_of_w, at:at + cols],
                                         start=(part_of_w == 0), stop=(part_of_w == PARTS - 1))
                    return last

                flips(0)
                pe.wait_ge(s_w, 1 if n == 0 else 2)
                for c in range(CHUNKS):
                    v = n * CHUNKS + c
                    if n == 0 and c == 2:
                        window_rows(1)
                    if c + 1 < CHUNKS:
                        flips(c + 1)
                    pe.wait_ge(s_hTc, 2 * (v + 1))
                    if v >= 2:
                        pe.wait_ge(s_yc, v - 1)
                    for j in range(CHUNK):
                        w = c * CHUNK + j
                        to = ps[6 + v % 2][:, j * WIDE:j * WIDE + (width if n < 3 else DIM)]
                        if n < 3:
                            last = product(to, v, j, WSTART[n], width)
                        else:
                            if w >= 2:
                                pe.wait_ge(s_stc[w % 2], (n - 3) * ((WINDOWS + 1 - w % 2) // 2) + w // 2)
                            product(ps[4 + w % 2][:, :], v, j, WSTART[n], RELS * DIM).then_inc(s_rooted, 1)
                            last = product(to, v, j, WSTART[n] + RELS * DIM, DIM)
                    last.then_inc(s_y, 1)

            def window_rows(n):
                pe.wait_ge(s_row, n)
                pe.matmul(ps[5][:, 0:GROUPS], ones[0:1, :], wrow[0:1, 2, :], start=True, stop=True).then_inc(s_rowb, 1)

            pe.wait_ge(s_const, 6)
            turn(0)
            pe.wait_ge(s_stat, 1)
            pe.transpose(ps[4][0:9, 0:P], stat[:, :], ident[:, :]).then_inc(s_statT, 1)
            pe.wait_ge(s_statD, 1)
            pe.matmul(ps[5][:, 0:9], ones[0:9, :], stD[:, :], start=True, stop=True).then_inc(s_statA, 1)
            window_rows(2)
            pe.wait_ge(s_runs, 1)
            runs = pe.value_load(runs_i[0:1, 0:1], min_val=1, max_val=RUNS)

            with pe.If(runs > 1):
                with pe.Fori(0, RUNS) as r:
                    with pe.Fori(0, GROUPS) as g:
                        for k in range(K):
                            pe.wait_ge(m_ready, (r * GROUPS + g) * K + k + 1)
                            for q in range(SPAN):
                                pe.matmul(ps[q][:, :], before_rings[:, q * P:(q + 1) * P],
                                          before_rings[:, 512:1024], start=True, stop=False)
                                last = pe.matmul(ps[q][:, :], before_rings[:, 256 + q * P:256 + (q + 1) * P],
                                                 before_rings[:, 1024:1536], start=False, stop=True)
                            last.then_inc(m_scored, 1)

            for p in passes:
                pe.wait_ge(p.begun, 1)
                pe.sem_inc(p.summed, SLOTS)
                if p.fetches:
                    pe.sem_inc(p.fetched, 2)

                def run(r, p=p):
                    def fetch(at, s):
                        pe.wait_ge(p.onehot, at + 1)
                        for c in range(FLIPS):
                            pe.wait_ge(p.flip_copied, at * FLIPS + c + 1)
                            for h in range(min(4, K - 4 * c)):
                                for q in range(SPAN):
                                    to = (h * SPAN + q) * P
                                    last = pe.transpose(flipb[c][:, to:to + P],
                                                        S[:, s % SLOTS, 4 * c + h, q * P:(q + 1) * P], identb[:, :])
                            last.then_inc(p.flipped, 1)
                        pe.wait_ge(p.flip_copied, (at + 1) * FLIPS + BANKS)
                        for k in range(K):
                            for q in range(SPAN):
                                last = pe.matmul(fetch_ps[s % 2][:, k * 24:(k + 1) * 24],
                                                 ST[:, s % 2, k, q * P:(q + 1) * P], tabw[:, s % 2, q, :],
                                                 start=(q == 0), stop=(q == SPAN - 1))
                        last.then_inc(p.fetched, 1)

                    def sums(at, i, s):
                        pe.wait_ge(p.weighted, at + 1)
                        v = PARTS * p.width + (RELS if p.kind == "count" else 0)
                        for q in range(SPAN):
                            for k in range(K):
                                last = pe.matmul(summed_ps[s % 2][:, q * 204:q * 204 + v],
                                                 S[:, s % SLOTS, k, q * P:(q + 1) * P], W3[:, s % 2, k, 0:v],
                                                 start=(k == 0), stop=(k == K - 1))
                        last.then_inc(p.summed, 1)

                    if p.fetches:
                        fetch(r * (GROUPS + 1), 0)
                    with pe.Fori(0, ITERS) as i:
                        for s in range(SLOTS):
                            if p.fetches:
                                fetch(r * (GROUPS + 1) + i * SLOTS + s + 1, s + 1)
                            sums(r * GROUPS + i * SLOTS + s, i, s)
                run(0)
                with pe.If(runs > 1):
                    with pe.Fori(1, RUNS) as r:
                        run(r)
                if p.kind == "count":
                    pe.wait_ge(s_hashed, 1)
                    pe.matmul(fetch_ps[0][:, 0:HASHES], ones[:, :], hsum[:, 0:HASHES],
                              start=True, stop=True).then_inc(s_hashsum, 1)
                    pe.wait_ge(s_turned, 1)
                    turned = pe.value_load(turned_i[0:1, 0:1], min_val=0, max_val=1)
                    with pe.If(turned > 0):
                        pe.sem_inc(backwards.summed, SLOTS)
                        with pe.Fori(0, RUNS) as r:
                            run(r, backwards)
                if p.n < 4:
                    turn(p.n + 1)

        @block.vector
        def _(dve):
            done = [0]

            def link(ins):
                done[0] += 1
                ins.then_inc(s_dve, 1)
                dve.wait_ge(s_dve, done[0])

            def bc(a, n):
                return a[:, :, None].to_broadcast((*a.shape, n)) if len(a.shape) == 2 else \
                    a[:, :, :, None].to_broadcast((*a.shape, n))

            def along(n, m=WINDOWS):
                return rows[:, n, :][:, None, :].to_broadcast((P, m, DIM))

            wide = acc[:, 0:WINDOWS, 0:DIM]
            norms = [0]

            def bch(a):
                return bc(a, DIM)

            def center(v):
                n = norms[0]
                norms[0] += 1
                for ws in HALVES:
                    link(dve.tensor_reduce(st[:, 0, ws], v[:, ws, :], AX.X, ALU.add))
                    link(dve.tensor_scalar(st[:, 0, ws], st[:, 0, ws], 1.0 / DIM, None, ALU.mult))
                    dve.tensor_tensor(tmp[:, ws, :], v[:, ws, :], bch(st[:, 0, ws]), ALU.subtract).then_inc(s_centered, 1)
                for h, ws in enumerate(HALVES):
                    dve.wait_ge(s_squared, 2 * n + h + 1)
                    dve.tensor_reduce(st[:, 1, ws], Y[:, ws, 0:DIM], AX.X, ALU.add).then_inc(s_var, 1)
                for h, ws in enumerate(HALVES):
                    dve.wait_ge(s_std, 2 * n + h + 1)
                    link(dve.reciprocal(st[:, 2, ws], st[:, 2, ws]))

            hs = [0]

            def split_h():
                n = hs[0]
                hs[0] += 1
                for h, ws in enumerate(HALVES):
                    dve.wait_ge(s_h1, 2 * n + h + 1)
                    dve.tensor_tensor(tmp[:, ws, :], Hn[:, ws, :], Hp[:, ws, DIM:2 * DIM],
                                      ALU.subtract).then_inc(s_hrest, 1)
                for h, ws in enumerate(HALVES):
                    dve.wait_ge(s_h2, 2 * n + h + 1)
                    dve.tensor_tensor(Hp[:, ws, 0:DIM], tmp[:, ws, :], Hp[:, ws, 2 * DIM:3 * DIM],
                                      ALU.subtract).then_inc(s_hparts, 1)

            def norm_relu(v):
                center(v)
                for ws in HALVES:
                    dve.scalar_tensor_tensor(out=Hn[:, ws, :], in0=tmp[:, ws, :], scalar=0.0, in1=bch(st[:, 2, ws]),
                                             op0=ALU.max, op1=ALU.mult).then_inc(s_h, 1)
                split_h()

            def copy_y(n, between=None):
                width = WIDE if n == 0 else DIM
                for c in range(CHUNKS):
                    v = n * CHUNKS + c
                    if n >= 3:
                        for j in range(CHUNK):
                            w = c * CHUNK + j
                            if w % 2 == 1:
                                u = (n - 3) * WINDOWS + w
                                dve.wait_ge(s_rooted, u + 1)
                                if u >= BANKS:
                                    dve.wait_ge(s_stage[u % BANKS], 16 * (u // BANKS))
                                dve.tensor_copy(stage[:, u % BANKS, :], ps[4 + w % 2][:, :]).then_inc(s_stc[1], 1)
                    dve.wait_ge(s_y, v + 1)
                    dve.tensor_copy(Y[:, c * CHUNK:(c + 1) * CHUNK, 0:width],
                                    ps[6 + v % 2][:, 0:CHUNK * WIDE].rearrange("p (w c) -> p w c", c=WIDE)[:, :, 0:width]
                                    ).then_inc(s_yc, 1)
                    if between and c in between:
                        between[c]()

            def split(v):
                link(dve.tensor_copy(tab[:, :, 0, :], v))
                link(dve.tensor_tensor(tres[:, :, :], v, tab[:, :, 0, :], ALU.subtract))
                link(dve.tensor_copy(tab[:, :, 1, :], tres[:, :, :]))
                link(dve.tensor_tensor(tab[:, :, 2, :], tres[:, :, :], tab[:, :, 1, :], ALU.subtract))

            def first_parts_of_w(a, b, rest):
                link(dve.tensor_copy(Wparts[:, 0, a:b], Wall[:, a:b]))
                link(dve.tensor_tensor(rest, Wall[:, a:b], Wparts[:, 0, a:b], ALU.subtract))

            def other_parts_of_w(a, b, rest):
                link(dve.tensor_copy(Wparts[:, 1, a:b], rest))
                link(dve.tensor_copy(Wparts[0:DIM, 2, a:b], Wparts[0:DIM, 0, a:b]))
                link(dve.tensor_tensor(Wparts[DIM:P, 2, a:b], rest[DIM:P], Wparts[DIM:P, 1, a:b], ALU.subtract))
                dve.sem_inc(s_w, 1)

            link(dve.memset(X[:, WINDOWS - 1, :], 0.0))
            dve.memset(srcF[:, COLS:], 0.0)
            dve.memset(relsrcF[:, COLS:], 0.0)
            dve.memset(rel0[:, COLS:], -1.0)
            dve.memset(wint[0:1, 0, GROUPS:], 0)
            dve.memset(attn[:, WINDOWS:, :], 0.0)
            link(dve.memset(amax[:, WINDOWS:, :], 0.0))
            dve.sem_inc(s_xtail, 1)
            dve.wait_ge(s_wts, 16 * 8)
            for n in range(2):
                link(dve.tensor_tensor(attw[:, n, :], att[:, n, :], W0[:, 0:DIM], ALU.mult))
                link(dve.tensor_reduce(W0[:, DIM + n * HEADS:DIM + (n + 1) * HEADS],
                                       attw[:, n, :].rearrange("p (h c) -> p h c", h=HEADS), AX.X, ALU.add))
            first_parts_of_w(0, WSTART[3], Wrest[:, 0:WSTART[3]])
            other_parts_of_w(0, WSTART[3], Wrest[:, 0:WSTART[3]])
            dve.wait_ge(s_x, 32)
            norm_relu(X[:, :, :])

            dve.wait_ge(s_const, 6)
            dve.wait_ge(s_edges, 64)
            dve.tensor_copy(iota[:, :], iota_i[:, :])
            dve.tensor_copy(iotab[:, :], iota_i[:, :])
            dve.tensor_copy(srcF[:, 0:COLS], srcI)
            dve.tensor_copy(typF[:, :], typI)
            link(dve.tensor_copy(dstF, dstI))
            dve.tensor_copy(relsrcF[:, 0:COLS], dstF)
            first = dstI[0:1, 0:COLS].rearrange("p (g k) -> p g k", k=K)[:, :, 0]
            link(dve.tensor_scalar(wint[0:1, 0, 0:GROUPS], first, 7, None, ALU.arith_shift_right))
            link(dve.tensor_copy(wrow[0:1, 0, :], wint[0:1, 0, 0:GROUPS]))
            link(dve.tensor_scalar(wrow[0:1, 1, :], wrow[0:1, 0, :], float(WINDOWS - SPAN), 0.0, ALU.min, ALU.max))
            link(dve.tensor_scalar(wrow[0:1, 2, :], wrow[0:1, 1, :], float(P), None, ALU.mult))
            dve.sem_inc(s_row, 1)

            def relative():
                link(dve.tensor_tensor(rel0[:, 0:COLS].rearrange("p (g k) -> p g k", k=K),
                                       dstF.rearrange("p (g k) -> p g k", k=K),
                                       bc(ps[5][:, 0:GROUPS], K), ALU.subtract))

            def to_windows():
                dve.wait_ge(s_rowb, 1)
                relative()

            def distances():
                link(dve.tensor_scalar(rel[:, 0:COLS], rel0[:, 0:COLS], -(SPAN * P - 1) / 2.0, None, ALU.add))
                link(dve.tensor_tensor(rel[:, 0:COLS], rel[:, 0:COLS], rel[:, 0:COLS], ALU.mult))

            def farthest():
                link(dve.tensor_reduce(stat[:, 0:1], rel[:, 0:COLS - 1], AX.X, ALU.max))
                link(dve.tensor_tensor(stat[0:LAST, 0:1], stat[0:LAST, 0:1], rel[0:LAST, COLS - 1:COLS], ALU.max))

            copy_y(0, {3: to_windows, 4: distances, 5: farthest})

            dve.wait_ge(s_yc, CHUNKS)
            a_src, a_dst = Y[:, :, DIM:DIM + HEADS], Y[:, :, DIM + HEADS:WIDE]
            link(dve.tensor_reduce(stat[:, 1:5], a_src.rearrange("p w h -> p h w"), AX.X, ALU.max))
            link(dve.tensor_reduce(stat[:, 5:9], a_src.rearrange("p w h -> p h w"), AX.X, ALU.min))
            link(dve.tensor_scalar(stat[:, 5:9], stat[:, 5:9], -1.0, None, ALU.mult))
            dve.sem_inc(s_stat, 1)
            dve.wait_ge(s_wr, 2 * (2 * BASES - 1))
            dve.wait_ge(s_wts3, 16 * 17)
            first_parts_of_w(WSTART[3], WCOLS, Wrest)
            dve.wait_ge(s_statT, 1)
            link(dve.tensor_reduce(stv[:, :], ps[4][0:9, 0:P], AX.X, ALU.max))
            link(dve.tensor_scalar(stD[:, :], ident[0:9, 0:9], stv[:, 0:1], None, ALU.mult))
            dve.sem_inc(s_statD, 1)
            other_parts_of_w(WSTART[3], WCOLS, Wrest)
            dve.wait_ge(s_statA, 1)
            link(dve.tensor_copy(stA[:, :], ps[5][:, 0:9]))
            link(dve.tensor_tensor(flag[:, 0:4], stA[:, 1:5], stA[:, 5:9], ALU.add))
            link(dve.tensor_reduce(flag[:, 4:5], flag[:, 0:4], AX.X, ALU.max))
            link(dve.tensor_scalar(flag[:, 5:6], flag[:, 4:5], RANGE, None, ALU.is_gt))
            link(dve.tensor_scalar(flag[:, 6:7], stA[:, 0:1], ((SPAN * P - 1) / 2.0) ** 2 + 1.0, None, ALU.is_gt))
            link(dve.tensor_tensor(flag[:, 7:8], flag[:, 5:6], flag[:, 6:7], ALU.max))
            link(dve.tensor_scalar(runs_i[0:1, :], flag[0:1, 7:8], float(RUNS - 1), 1.0, ALU.mult, ALU.add))
            dve.sem_inc(s_runs, 1)
            dve.sem_inc(passes[0].begun, 1)
            link(dve.tensor_scalar(flag[0:1, 0:1], flag[0:1, 7:8], -1.0, 1.0, ALU.mult, ALU.add))
            link(dve.tensor_scalar(wrow[0:1, 1, :], wrow[0:1, 1, :], flag[0:1, 0:1], None, ALU.mult))
            link(dve.tensor_copy(wint[0:1, 0, 0:GROUPS], wrow[0:1, 1, :]))
            link(dve.tensor_scalar(wrow[0:1, 2, :], wrow[0:1, 1, :], float(P), None, ALU.mult))
            dve.sem_inc(s_row, 1)
            dve.wait_ge(s_rowb, 2)
            relative()
            link(dve.tensor_copy(amax[:, 0:WINDOWS, :], stA[:, 1:5][:, None, :].to_broadcast((P, WINDOWS, HEADS))))
            runs = dve.value_load(runs_i[0:1, 0:1], min_val=1, max_val=RUNS)

            def start_windows():
                dve.tensor_copy(rel[:, :], rel0[:, :])
                link(dve.tensor_copy(wint[0:1, 1, :], wint[0:1, 0, :]))

            start_windows()
            with dve.If(runs > 1):
                mine = [0]

                def mlink(ins, at):
                    mine[0] += 1
                    ins.then_inc(m_step, 1)
                    dve.wait_ge(m_step, at + mine[0])

                Sf, Sn = before_rings[:, 0:256], before_rings[:, 256:512]
                Dg = before_rings[:, 512:1024].rearrange("p (h e) -> p h e", h=HEADS)
                Ii = before_rings[:, 1024:1536].rearrange("p (h e) -> p h e", h=HEADS)
                four = ident[:, None, :].to_broadcast((P, HEADS, P))
                mlink(dve.tensor_copy(Ii, four), 0)
                mlink(dve.tensor_copy(amax[:, 0:WINDOWS, :], a_src), 0)
                before = mine[0]
                STEPS = K * (2 + 2 * SPAN)
                with dve.Fori(0, RUNS) as r:
                    with dve.Fori(0, GROUPS) as g:
                        n = r * GROUPS + g
                        dve.wait_ge(m_gathered, (n + 1) * (K * 16))
                        w = dve.value_load(wint[0:1, 1, bass.ds(g, 1)], min_val=0, max_val=WPAD - SPAN)
                        mine[0] = before
                        at = n * STEPS + r * 2
                        for k in range(K):
                            mlink(dve.tensor_scalar(Sf, iota[:, :], rel[:, bass.ds(g * K + k, 1)], None,
                                                    ALU.is_equal), at)
                            dve.tensor_tensor(Dg, four, bc(G[:, 0, k, DIM:DIM + HEADS], P), ALU.mult)
                            mlink(dve.tensor_scalar(Sn, Sf, -1.0, BIG, ALU.add, ALU.mult), at)
                            dve.sem_inc(m_ready, 1)
                            dve.wait_ge(m_scored, n * K + k + 1)
                            for q in range(SPAN):
                                mlink(dve.tensor_reduce(sc[:, 0, 0:HEADS],
                                                        ps[q][:, :].rearrange("p (h e) -> p h e", h=HEADS),
                                                        AX.X, ALU.max), at)
                                to = amax[:, bass.ds(w + q, 1), :].rearrange("p a h -> p (a h)")
                                mlink(dve.tensor_tensor(to, to, sc[:, 0, 0:HEADS], ALU.max), at)
                            dve.sem_inc(m_taken, 1)
                    mine[0] = before
                    at = (r + 1) * (GROUPS * STEPS) + r * 2
                    mlink(dve.tensor_scalar(rel[:, :], rel[:, :], -float(SPAN * P), None, ALU.add), at)
                    mlink(dve.tensor_scalar(wint[0:1, 1, :], wint[0:1, 1, :], SPAN, None, ALU.add), at)
                    dve.sem_inc(s_maxed, 1)

            start_windows()
            link(dve.tensor_copy(attn[:, 0:WINDOWS, 0:HEADS], a_dst))
            link(dve.tensor_tensor(ns[:, 0, 0:WINDOWS, :], amax[:, 0:WINDOWS, :], a_dst, ALU.add))
            link(dve.scalar_tensor_tensor(out=attn[:, 0:WINDOWS, HEADS:8], in0=ns[:, 0, 0:WINDOWS, :], scalar=SLOPE,
                                          in1=ns[:, 0, 0:WINDOWS, :], op0=ALU.mult, op1=ALU.max))
            split(attn[:, :, :])

            def residue(step, v, q):
                step(dve.tensor_scalar(q, v, 1.0 / PRIME, ROUND, ALU.mult, ALU.add))
                step(dve.tensor_scalar(q, q, -ROUND, -float(PRIME), ALU.add, ALU.mult))
                step(dve.tensor_tensor(v, v, q, ALU.add))

            HASH_STEPS = 2 + HASHES + 5 * 3 + 4 + 2

            def hash_edges(step, i):
                cols = bass.ds(i * HEDGES, HEDGES)
                step(dve.tensor_copy(ends[:, 0:HEDGES], srcF[:, cols]))
                step(dve.tensor_copy(ends[:, HEDGES:HCOLS], relsrcF[:, cols]))
                for n in range(HASHES):
                    step(dve.tensor_scalar(hx[:, n * HCOLS:(n + 1) * HCOLS], ends, HASH_SCALES[n], HASH_OFFSETS[n],
                                           ALU.mult, ALU.add))
                residue(step, hx, hq)
                step(dve.tensor_tensor(hx2, hx, hx, ALU.mult))
                residue(step, hx2, hq)
                step(dve.tensor_tensor(hx, hx, hx2, ALU.mult))
                residue(step, hx, hq)
                step(dve.tensor_tensor(hx2, hx2, hx2, ALU.mult))
                residue(step, hx2, hq)
                g = hx.rearrange("p (n e c) -> p n e c", n=HASHES, e=2)
                k = hx2.rearrange("p (n e c) -> p n e c", n=HASHES, e=2)
                q = hq.rearrange("p (n e c) -> p n e c", n=HASHES, e=2)
                total = hsum.rearrange("p (n c) -> p n c", n=HASHES)
                dve.tensor_tensor(q[:, :, 0, :], g[:, :, 0, :], k[:, :, 1, :], ALU.mult)
                step(dve.tensor_tensor(q[:, :, 1, :], g[:, :, 1, :], k[:, :, 0, :], ALU.mult))
                residue(step, hq, hx)
                step(dve.tensor_tensor(q[:, :, 0, :], q[:, :, 0, :], q[:, :, 1, :], ALU.subtract))
                step(dve.tensor_tensor(total, total, q[:, :, 0, :], ALU.add))

            def edge_pass(p):
                hashes = p is passes[1]
                PER_ITER = SLOTS * (3 + {"attention": 4, "relation": 4, "count": 0, "weight": 0}[p.kind]) \
                    + (2 * HASH_STEPS if hashes else 0)
                PER_RUN = ITERS * PER_ITER + 3

                def run(r):
                    steps, base = [0], [0]

                    def plink(ins):
                        steps[0] += 1
                        ins.then_inc(p.step, 1)
                        dve.wait_ge(p.step, base[0] + steps[0])

                    def window(at):
                        return dve.value_load(wint[0:1, 1, bass.ds(at, 1)], min_val=0, max_val=WPAD - SPAN)

                    def one_hot(at, s, w):
                        if p.fetches:
                            dve.tensor_copy(tabw[:, s % 2, :, :],
                                            tab[:, bass.ds(w, SPAN), :, :].rearrange("p w a c -> p w (a c)"))
                        plink(dve.tensor_copy(relw[:, s % SLOTS, :], rel[:, bass.ds(at * K, K)]))
                        for k in range(K):
                            last = dve.tensor_scalar(S[:, s % SLOTS, k, :], iotab[:, :], relw[:, s % SLOTS, k:k + 1], None,
                                                     ALU.is_equal)
                        last.then_inc(p.onehot, 1)

                    def weigh(i, s, load_windows):
                        num = r * GROUPS + i * SLOTS + s
                        cols = bass.ds((i * SLOTS + s) * K, K)
                        if p.fetches:
                            dve.wait_ge(p.fetched, r * (GROUPS + 1) + i * SLOTS + s + 1 + 2)
                            three = fetch_ps[s % 2][:, 0:24 * K].rearrange("p (k a c) -> p k c a", k=K, a=3)
                            plink(dve.tensor_reduce(f1[:, :, :], three, AX.X, ALU.add))
                        if p.kind == "relation":
                            plink(dve.tensor_tensor(sc[:, :, :],
                                                    iota[:, 0:RELS][:, None, :].to_broadcast((P, K, RELS)),
                                                    bc(typF[:, cols], RELS), ALU.is_equal))
                            plink(dve.tensor_tensor(sc[:, :, :], sc[:, :, :], f1[:, :, :], ALU.mult))
                            plink(dve.tensor_reduce(wt[:, :], sc[:, :, :], AX.X, ALU.add))
                        dve.wait_ge(p.gathered[s], (r * ITERS + i + 1) * (K * 16))
                        v = p.width
                        if p.kind == "attention":
                            plink(dve.tensor_tensor(sc[:, :, 0:HEADS], G[:, s, :, DIM:DIM + HEADS],
                                                    f1[:, :, 0:HEADS], ALU.add))
                            plink(dve.scalar_tensor_tensor(out=sc[:, :, HEADS:8], in0=sc[:, :, 0:HEADS],
                                                           scalar=SLOPE, in1=sc[:, :, 0:HEADS],
                                                           op0=ALU.mult, op1=ALU.max))
                            plink(dve.tensor_tensor(sc[:, :, 0:HEADS], sc[:, :, HEADS:8],
                                                    f1[:, :, HEADS:8], ALU.subtract))
                            dve.tensor_scalar(sc[:, :, 0:HEADS], sc[:, :, 0:HEADS], 0.0, None,
                                              ALU.min).then_inc(p.exp_in, 1)
                            dve.wait_ge(p.exp_out, num + 1)
                            dve.tensor_tensor(
                                Wf[:, :, 0:DIM].rearrange("p k (h c) -> p k h c", h=HEADS),
                                G[:, s, :, 0:DIM].rearrange("p k (h c) -> p k h c", h=HEADS),
                                bc(Wf[:, :, DIM:DIM + HEADS], CH), ALU.mult).then_inc(p.whole, 1)
                        elif p.kind == "count":
                            dve.tensor_tensor(W3[:, s % 2, :, PARTS * DIM:PARTS * DIM + RELS],
                                              iota[:, 0:RELS][:, None, :].to_broadcast((P, K, RELS)),
                                              bc(typF[:, cols], RELS), ALU.is_equal).then_inc(p.whole, 1)
                        else:
                            weight = wt[:, :] if p.kind == "relation" else ew[:, cols]
                            dve.tensor_tensor(Wf[:, :, 0:DIM], G[:, s, :, 0:DIM],
                                              bc(weight, DIM), ALU.mult).then_inc(p.whole, 1)
                        load_windows(s)
                        dve.wait_ge(p.high, num + 1)
                        weighted = G[:, s, :, 0:v] if p.kind == "count" else Wf[:, :, 0:v]
                        dve.tensor_tensor(Rf[:, :, 0:v], weighted, W3[:, s % 2, :, 0:v],
                                          ALU.subtract).then_inc(p.rest, 1)
                        dve.wait_ge(p.middle, num + 1)
                        dve.tensor_tensor(W3[:, s % 2, :, 2 * v:3 * v], Rf[:, :, 0:v], W3[:, s % 2, :, v:2 * v],
                                          ALU.subtract).then_inc(p.weighted, 1)

                    def add(i, s, w):
                        dve.wait_ge(p.summed, r * GROUPS + i * SLOTS + s + 1 + SLOTS)
                        v = p.width
                        got = summed_ps[s % 2][:, 0:SPAN * 204].rearrange("p (q c) -> p q c", q=SPAN)
                        sub = part[:, :, 0:v]
                        if p.kind == "count":
                            to = acc[:, bass.ds(w, SPAN), DIM:WIDE]
                            dve.tensor_tensor(to, to, got[:, :, PARTS * DIM:PARTS * DIM + RELS], ALU.add)
                        plink(dve.tensor_reduce(
                            sub, got[:, :, 0:3 * v].rearrange("p q (a c) -> p q c a", a=PARTS), AX.X, ALU.add))
                        to = acc[:, bass.ds(w, SPAN), 0:v]
                        plink(dve.tensor_tensor(to, to, sub, ALU.add))

                    if not isinstance(r, int):
                        dve.tensor_scalar(rel[:, :], rel[:, :], -float(SPAN * P), None, ALU.add).then_inc(p.step, 1)
                        dve.tensor_scalar(wint[0:1, 1, :], wint[0:1, 1, :], SPAN, None, ALU.add).then_inc(p.step, 1)
                        dve.wait_ge(p.step, r * PER_RUN + p.before)
                        dve.wait_ge(p.idx_ready, r * (GROUPS + SLOTS))
                        dve.sem_inc(p.begun, 1)
                    base[0] = r * PER_RUN + p.before
                    one_hot(0, 0, window(0))
                    with dve.Fori(0, ITERS) as i:
                        base[0], steps[0] = r * PER_RUN + i * PER_ITER + p.before, 1
                        ws = {1: window(i * SLOTS + 1)}

                        def load_windows(s):
                            if s == 0:
                                ws[0] = window(i * SLOTS)
                            if s + 2 <= SLOTS:
                                ws[s + 2] = window(i * SLOTS + s + 2)

                        for s in range(SLOTS):
                            one_hot(i * SLOTS + s + 1, s + 1, ws[s + 1])
                            weigh(i, s, load_windows)
                            if s > 0:
                                add(i, s - 1, ws[s - 1])
                            if hashes and s % 2 == 1:
                                hash_edges(plink, i * 2 + s // 2)
                        add(i, SLOTS - 1, ws[SLOTS - 1])
                        assert steps[0] == 1 + PER_ITER

                def other_runs():
                    with dve.Fori(1, RUNS) as r:
                        run(r)
                    dve.wait_ge(p.idx_ready, RUNS * (GROUPS + SLOTS))
                    dve.tensor_copy(rel[:, :], rel0[:, :]).then_inc(p.step, 1)
                    dve.tensor_copy(wint[0:1, 1, :], wint[0:1, 0, :]).then_inc(p.step, 1)
                    dve.wait_ge(p.step, RUNS * PER_RUN + p.before)

                run(0)
                if p is backwards:
                    other_runs()
                    return
                with dve.If(runs > 1):
                    other_runs()
                dve.wait_ge(p.idx_ready, GROUPS + SLOTS)
                if p.n in (0, 2, 3):
                    dve.sem_inc(passes[p.n + 1].begun, 1)

            link(dve.tensor_tensor(ns[:, 0, 0:WINDOWS, :], a_src, a_dst, ALU.add))
            link(dve.scalar_tensor_tensor(out=ns[:, 1, 0:WINDOWS, :], in0=ns[:, 0, 0:WINDOWS, :], scalar=SLOPE,
                                          in1=ns[:, 0, 0:WINDOWS, :], op0=ALU.mult, op1=ALU.max))
            link(dve.tensor_tensor(ns[:, 0, 0:WINDOWS, :], ns[:, 1, 0:WINDOWS, :], attn[:, 0:WINDOWS, HEADS:8],
                                   ALU.subtract))
            dve.sem_inc(s_self, 1)
            link(dve.tensor_tensor(Hn[:, :, :], Hn[:, :, :], along(0), ALU.add))
            dve.wait_ge(s_pself, 1)
            pself = ns[:, 1, 0:WINDOWS, :]
            w4d = wide.rearrange("p w (h c) -> p w h c", h=HEADS)
            dve.tensor_tensor(w4d, Y[:, :, 0:DIM].rearrange("p w (h c) -> p w h c", h=HEADS), bc(pself, CH), ALU.mult)
            dve.memset(acc[:, WINDOWS:, :], 0.0)
            link(dve.tensor_copy(acc[:, 0:WINDOWS, DIM:DIM + HEADS], pself))
            link(dve.tensor_tensor(X[:, :, :], X[:, :, :], along(2), ALU.add))
            edge_pass(passes[0])
            link(dve.reciprocal(ns[:, 0, 0:WINDOWS, :], acc[:, 0:WINDOWS, DIM:DIM + HEADS]))
            t4d = tmp[:, :, :].rearrange("p w (h c) -> p w h c", h=HEADS)
            link(dve.tensor_tensor(t4d, w4d, bc(ns[:, 0, 0:WINDOWS, :], CH), ALU.mult))
            link(dve.tensor_tensor(Hn[:, :, :], Hn[:, :, :], tmp[:, :, :], ALU.add))
            center(Hn[:, :, :])
            link(dve.tensor_tensor(tmp[:, :, :], tmp[:, :, :], bch(st[:, 2, :]), ALU.mult))
            link(dve.tensor_tensor(tmp[:, :, :], tmp[:, :, :], along(1), ALU.mult))
            link(dve.tensor_tensor(X[:, :, :], X[:, :, :], tmp[:, :, :], ALU.add))

            norm_relu(X[:, :, :])
            copy_y(1)
            dve.wait_ge(s_yc, 2 * CHUNKS)
            dve.tensor_copy(wide, Y[:, :, 0:DIM])
            link(dve.memset(acc[:, :, DIM:WIDE], 0.0))
            dve.memset(hsum, 0.0)
            link(dve.tensor_tensor(X[:, :, :], X[:, :, :], along(3), ALU.add))
            edge_pass(passes[1])
            residue(link, hsum, hq[:, 0:HASHES * HEDGES])
            link(dve.tensor_reduce(hq[:, 0:HASHES], hsum.rearrange("p (n c) -> p n c", n=HASHES), AX.X, ALU.add))
            residue(link, hq[:, 0:HASHES], hx[:, 0:HASHES])
            link(dve.tensor_copy(hsum[:, 0:HASHES], hq[:, 0:HASHES]))
            dve.sem_inc(s_hashed, 1)
            link(dve.tensor_scalar(attn[:, :, :], acc[:, :, DIM:WIDE], 1.0, None, ALU.max))
            dve.wait_ge(s_hashsum, 1)
            link(dve.tensor_copy(hq[:, 0:HASHES], fetch_ps[0][:, 0:HASHES]))
            residue(link, hq[:, 0:HASHES], hx[:, 0:HASHES])
            link(dve.tensor_tensor(hq[:, 0:HASHES], hq[:, 0:HASHES], hq[:, 0:HASHES], ALU.mult))
            link(dve.tensor_reduce(hx[:, 0:1], hq[:, 0:HASHES], AX.X, ALU.max))
            link(dve.tensor_scalar(turned_i[0:1, :], hx[0:1, 0:1], 1.0, None, ALU.min))
            dve.sem_inc(s_turned, 1)
            turned = dve.value_load(turned_i[0:1, 0:1], min_val=0, max_val=1)
            with dve.If(turned > 0):
                dve.tensor_copy(rel[:, 0:COLS], srcF[:, 0:COLS]).then_inc(backwards.step, 1)
                dve.tensor_scalar(wint[0:1, 1, :], wint[0:1, 1, :], 0, None, ALU.mult).then_inc(backwards.step, 1)
                dve.memset(acc[:, :, DIM:WIDE], 0.0)
                dve.tensor_copy(wide, Y[:, :, 0:DIM]).then_inc(backwards.step, 1)
                dve.wait_ge(backwards.step, backwards.before)
                dve.sem_inc(backwards.begun, 1)
                edge_pass(backwards)
            link(dve.tensor_reduce(st[:, 2, :], acc[:, 0:WINDOWS, DIM:WIDE], AX.X, ALU.add))
            link(dve.tensor_scalar(st[:, 0, :], st[:, 2, :], 1.0, 1.0, ALU.add, ALU.max))
            dve.sem_inc(s_self, 1)
            dve.sem_inc(passes[2].begun, 1)
            dve.wait_ge(s_pself, 2)
            link(dve.reciprocal(st[:, 0, :], st[:, 1, :]))
            link(dve.tensor_tensor(tmp[:, :, :], wide, bch(st[:, 0, :]), ALU.mult))
            link(dve.tensor_tensor(X[:, :, :], X[:, :, :], tmp[:, :, :], ALU.add))

            norm_relu(X[:, :, :])
            def rows_by_relation():
                dve.scalar_tensor_tensor(out=relsrcF[:, 0:COLS], in0=srcF[:, 0:COLS], scalar=float(RELS),
                                         in1=typF[:, :], op0=ALU.mult, op1=ALU.add)

            rows_by_relation()
            copy_y(2)
            link(dve.reciprocal(attn[:, :, :], attn[:, :, :]))
            link(dve.tensor_tensor(wide, X[:, :, :], along(4), ALU.add))
            link(dve.memset(acc[:, WINDOWS:, :], 0.0))
            split(attn[:, :, :])
            dve.wait_ge(s_yc, 3 * CHUNKS)
            edge_pass(passes[2])

            norm_relu(wide)
            copy_y(3)
            dve.tensor_tensor(X[:, :, :], wide, along(6), ALU.add)
            dve.wait_ge(s_yc, 4 * CHUNKS)
            link(dve.tensor_tensor(tmp[:, :, :], Y[:, :, 0:DIM], along(5), ALU.add))
            link(dve.tensor_copy(wide, tmp[:, :, :]))
            for b in range(BANKS):
                dve.wait_ge(s_stage[b], 16 * len(range(b, WINDOWS, BANKS)))
            edge_pass(passes[3])
            for ws in HALVES:
                dve.tensor_scalar(Hn[:, ws, :], wide[:, ws, :], 0.0, None, ALU.max).then_inc(s_h, 1)
            split_h()
            copy_y(4)
            dve.wait_ge(s_yc, 5 * CHUNKS)
            link(dve.tensor_tensor(wide, X[:, :, :], Y[:, :, 0:DIM], ALU.add))
            for b in range(BANKS):
                dve.wait_ge(s_stage[b], 16 * len(range(b, 2 * WINDOWS, BANKS)))
            edge_pass(passes[4])
            dve.sem_inc(s_out, 1)


_INS = ['x', 'src', 'dst', 'edge_type_8', 'edge_weight', 'L0_gnn_W', 'L0_gnn_att_src', 'L0_gnn_att_dst',
        'L0_gnn_bias', 'L0_gnn_gamma', 'L0_gnn_beta', 'L1_gnn_weight', 'L1_gnn_bias', 'L2_gnn_W', 'L2_gnn_b',
        'L3_gnn_basis1', 'L3_gnn_comp1', 'L3_gnn_root1', 'L3_gnn_bias1', 'L3_gnn_basis2', 'L3_gnn_comp2',
        'L3_gnn_root2', 'L3_gnn_bias2']


def kernel(**inputs):
    import numpy as _np
    import concourse.bacc as _bacc
    from concourse import mybir as _mybir
    from concourse.bass_utils import run_bass_kernel_spmd as _run

    def by_column(a, fill):
        full = _np.full(COLS * P, fill, a.dtype)
        full[:EDGES] = a
        return full.reshape(COLS, P).T

    nc = _bacc.Bacc("TRN2", target_bir_lowering=False, num_devices=1)
    arrays, args = {}, []
    for name in _INS:
        a = _np.asarray(inputs[name])
        if name in ("src", "dst"):
            a = by_column(a, PADNODE)
        if name in ("edge_type_8", "edge_weight"):
            a = by_column(a, 0)
        if name in ("L1_gnn_weight", "L2_gnn_W"):
            a = a.T
        a = _np.ascontiguousarray(a)
        arrays[f"in_{name}"] = a
        args.append(nc.dram_tensor(f"in_{name}", a.shape, _mybir.dt.from_np(a.dtype), kind="ExternalInput").ap())
    args.append(nc.dram_tensor("out_x", (NODES, DIM), _mybir.dt.float32, kind="ExternalOutput").ap())
    gnn_stack(nc, *args)
    r = _run(nc, [arrays], core_ids=[0])
    return r.results[0]["out_x"]
```
